# Optimizing a Trainium2 kernel written in Bass

```python
import numpy as np
import jax
import jax.numpy as jnp

def _softmax(x, axis=-1):
    return jax.nn.softmax(x, axis=axis)

def _gelu(x):
    return jax.nn.gelu(x, approximate=True)

def _silu(x):
    return jax.nn.silu(x)

def _sigmoid(x):
    return jax.nn.sigmoid(x)

def _layernorm(x, axis=-1, eps=1e-05):
    m = jnp.mean(x, axis=axis, keepdims=True)
    v = jnp.var(x, axis=axis, keepdims=True)
    return (x - m) / jnp.sqrt(v + eps)

def _scatter_add(tgt, idx, src, axis=0):
    return tgt.at[idx].add(src)

def _segment_sum(src, seg, n):
    return jax.ops.segment_sum(src, seg, n)
kernel_name = 'mk_flamingo_gated_d1_seqx_r4_a17bca'

def setup_inputs(seed: int=0):
    np.random.seed(seed)
    _w = jnp.asarray

    def _rec_inputs():
        import jax
        import jax.numpy as jnp
        _rk = jax.random.key(seed)
        x = 6.313e-05 + 0.9998 * jax.random.normal(jax.random.fold_in(_rk, 1), (32, 128, 256), jnp.float32)
        _lenS = 128 - jax.random.randint(jax.random.fold_in(_rk, 7), (32,), 0, max(1, 128 // 4) + 1, jnp.int32)
        _lenS2 = 128 - jax.random.randint(jax.random.fold_in(_rk, 8), (32,), 0, max(1, 128 // 4) + 1, jnp.int32)
        _ctx_1024P = jax.random.normal(jax.random.fold_in(_rk, 11), (32, 16, 256), jnp.float32)
        _ctx_1024c = jax.random.dirichlet(jax.random.fold_in(_rk, 511), 0.3 * jnp.ones((16,), jnp.float32), (32, 128))
        _ctx_1024t = jnp.einsum('bsk,bkd->bsd', _ctx_1024c, _ctx_1024P)
        _ctx_1024t = _ctx_1024t * jax.lax.rsqrt(jnp.mean(jnp.square(_ctx_1024t)) + 1e-12) * 0.953939
        ctx_1024 = -0.000214406 + 1.00034 * (_ctx_1024t + 0.3 * jax.random.normal(jax.random.fold_in(_rk, 611), (32, 128, 256), jnp.float32))
        _g = jax.random.normal(jax.random.fold_in(_rk, 9001), (2, 1), jnp.float32)
        _g = jnp.sign(_g) * jnp.maximum(jnp.abs(_g), 1.0) + (_g == 0) * 1.0
        g_xattn = _g[0]
        g_ffn = _g[1]
        return (x, ctx_1024, g_xattn, g_ffn)
    x, ctx_1024, g_xattn, g_ffn = _rec_inputs()

    def _L0_xattn_setup():
        import jax, jax.numpy as jnp
        import numpy as np
        from jax import lax
        BIG = jnp.float32(1e+30)

        def _pairwise_euclidean(a, b):
            aa = jnp.sum(a * a, axis=-1)[:, None]
            bb = jnp.sum(b * b, axis=-1)[None, :]
            ab = a @ b.T
            return jnp.sqrt(jnp.maximum(aa + bb - 2.0 * ab, 0.0))

        def _dtw_cost(D):
            row0 = jnp.cumsum(D[0])

            def row_step(prev_row, d_row):
                first = d_row[0] + prev_row[0]

                def col_step(left, inp):
                    d_ij, up, diag = inp
                    r = d_ij + jnp.minimum(jnp.minimum(up, left), diag)
                    return (r, r)
                _, rest = lax.scan(col_step, first, (d_row[1:], prev_row[1:], prev_row[:-1]))
                row = jnp.concatenate([first[None], rest])
                return (row, row)
            _, rows = lax.scan(row_step, row0, D[1:])
            return jnp.concatenate([row0[None], rows], axis=0)

        def _backtrack(R, T1, T2):
            L = T1 + T2 - 1

            def step(carry, _):
                i, j, done = carry
                valid = jnp.logical_not(done)
                cd = jnp.where((i > 0) & (j > 0), R[jnp.maximum(i - 1, 0), jnp.maximum(j - 1, 0)], BIG)
                cu = jnp.where(i > 0, R[jnp.maximum(i - 1, 0), j], BIG)
                cl = jnp.where(j > 0, R[i, jnp.maximum(j - 1, 0)], BIG)
                choice = jnp.argmin(jnp.stack([cd, cu, cl]))
                ni = jnp.where(choice <= 1, i - 1, i)
                nj = jnp.where((choice == 0) | (choice == 2), j - 1, j)
                at_origin = (i == 0) & (j == 0)
                ni = jnp.where(at_origin, 0, ni)
                nj = jnp.where(at_origin, 0, nj)
                return ((ni, nj, done | at_origin), (i, j, valid))
            init = (jnp.int32(T1 - 1), jnp.int32(T2 - 1), jnp.bool_(False))
            _, (i_idx, j_idx, valid) = lax.scan(step, init, None, length=L)
            return (i_idx, j_idx, valid)

        def _align_one(small, large):
            T_small, d = small.shape
            T_large = large.shape[0]
            D = _pairwise_euclidean(small, large)
            R = _dtw_cost(D)
            i_idx, j_idx, valid = _backtrack(R, T_small, T_large)
            contrib = small[i_idx] * valid[:, None].astype(small.dtype)
            expanded = jnp.zeros((T_large, d), dtype=small.dtype).at[j_idx].add(contrib)
            return expanded
        key = jax.random.key(seed)
        k1, k2 = jax.random.split(key)
        teacher = jax.random.normal(k1, (16, 100, 256), dtype=jnp.float32)
        student = jax.random.normal(k2, (16, 150, 256), dtype=jnp.float32)
        return {'teacher_features': teacher, 'student_features': student}
    _L0_xattn_all = _L0_xattn_setup()
    _L0_xattn_in = {k: v for k, v in _L0_xattn_all.items() if k in ()}
    del _L0_xattn_all

    def _L0_ffn_setup():
        import jax, jax.numpy as jnp
        import numpy as np
        E = 8
        K = 2
        key = jax.random.key(seed)
        ks = jax.random.split(key, 8)
        B, T, d = (4, 512, 256)
        h = 4 * d // E
        s = 0.02
        X = jax.random.normal(ks[0], (B, T, d), jnp.float32)
        routing_W = jax.random.normal(ks[1], (E, d), jnp.float32) * s
        expert_bias = jnp.zeros((E,), jnp.float32)
        sW1 = jax.random.normal(ks[2], (d, h), jnp.float32) * s
        sb1 = jnp.zeros((h,), jnp.float32)
        sW2 = jax.random.normal(ks[3], (h, d), jnp.float32) * s
        sb2 = jnp.zeros((d,), jnp.float32)
        rW1 = jax.random.normal(ks[4], (E, d, h), jnp.float32) * s
        rb1 = jnp.zeros((E, h), jnp.float32)
        rW2 = jax.random.normal(ks[5], (E, h, d), jnp.float32) * s
        rb2 = jnp.zeros((E, d), jnp.float32)
        return dict(X=X, routing_W=routing_W, expert_bias=expert_bias, sW1=sW1, sb1=sb1, sW2=sW2, sb2=sb2, rW1=rW1, rb1=rb1, rW2=rW2, rb2=rb2)
    _L0_ffn_all = _L0_ffn_setup()
    _L0_ffn_in = {k: v for k, v in _L0_ffn_all.items() if k in ('routing_W', 'expert_bias', 'sW1', 'sb1', 'sW2', 'sb2', 'rW1', 'rb1', 'rW2', 'rb2')}
    del _L0_ffn_all
    return {'x': x, 'ctx_1024': ctx_1024, 'g_xattn': g_xattn, 'g_ffn': g_ffn, 'L0_ffn_routing_W': _L0_ffn_in['routing_W'], 'L0_ffn_expert_bias': _L0_ffn_in['expert_bias'], 'L0_ffn_sW1': _L0_ffn_in['sW1'], 'L0_ffn_sb1': _L0_ffn_in['sb1'], 'L0_ffn_sW2': _L0_ffn_in['sW2'], 'L0_ffn_sb2': _L0_ffn_in['sb2'], 'L0_ffn_rW1': _L0_ffn_in['rW1'], 'L0_ffn_rb1': _L0_ffn_in['rb1'], 'L0_ffn_rW2': _L0_ffn_in['rW2'], 'L0_ffn_rb2': _L0_ffn_in['rb2']}

def reference(x, ctx_1024, g_xattn, g_ffn, L0_ffn_routing_W, L0_ffn_expert_bias, L0_ffn_sW1, L0_ffn_sb1, L0_ffn_sW2, L0_ffn_sb2, L0_ffn_rW1, L0_ffn_rb1, L0_ffn_rW2, L0_ffn_rb2):
    import jax
    import jax.numpy as jnp

    def _L0_xattn_ref(teacher_features, student_features):
        import jax, jax.numpy as jnp
        import numpy as np
        from jax import lax
        BIG = jnp.float32(1e+30)

        def _pairwise_euclidean(a, b):
            aa = jnp.sum(a * a, axis=-1)[:, None]
            bb = jnp.sum(b * b, axis=-1)[None, :]
            ab = a @ b.T
            return jnp.sqrt(jnp.maximum(aa + bb - 2.0 * ab, 0.0))

        def _dtw_cost(D):
            row0 = jnp.cumsum(D[0])

            def row_step(prev_row, d_row):
                first = d_row[0] + prev_row[0]

                def col_step(left, inp):
                    d_ij, up, diag = inp
                    r = d_ij + jnp.minimum(jnp.minimum(up, left), diag)
                    return (r, r)
                _, rest = lax.scan(col_step, first, (d_row[1:], prev_row[1:], prev_row[:-1]))
                row = jnp.concatenate([first[None], rest])
                return (row, row)
            _, rows = lax.scan(row_step, row0, D[1:])
            return jnp.concatenate([row0[None], rows], axis=0)

        def _backtrack(R, T1, T2):
            L = T1 + T2 - 1

            def step(carry, _):
                i, j, done = carry
                valid = jnp.logical_not(done)
                cd = jnp.where((i > 0) & (j > 0), R[jnp.maximum(i - 1, 0), jnp.maximum(j - 1, 0)], BIG)
                cu = jnp.where(i > 0, R[jnp.maximum(i - 1, 0), j], BIG)
                cl = jnp.where(j > 0, R[i, jnp.maximum(j - 1, 0)], BIG)
                choice = jnp.argmin(jnp.stack([cd, cu, cl]))
                ni = jnp.where(choice <= 1, i - 1, i)
                nj = jnp.where((choice == 0) | (choice == 2), j - 1, j)
                at_origin = (i == 0) & (j == 0)
                ni = jnp.where(at_origin, 0, ni)
                nj = jnp.where(at_origin, 0, nj)
                return ((ni, nj, done | at_origin), (i, j, valid))
            init = (jnp.int32(T1 - 1), jnp.int32(T2 - 1), jnp.bool_(False))
            _, (i_idx, j_idx, valid) = lax.scan(step, init, None, length=L)
            return (i_idx, j_idx, valid)

        def _align_one(small, large):
            T_small, d = small.shape
            T_large = large.shape[0]
            D = _pairwise_euclidean(small, large)
            R = _dtw_cost(D)
            i_idx, j_idx, valid = _backtrack(R, T_small, T_large)
            contrib = small[i_idx] * valid[:, None].astype(small.dtype)
            expanded = jnp.zeros((T_large, d), dtype=small.dtype).at[j_idx].add(contrib)
            return expanded
        return jax.vmap(_align_one)(teacher_features, student_features)

    def _L0_ffn_ref(X, routing_W, expert_bias, sW1, sb1, sW2, sb2, rW1, rb1, rW2, rb2):
        import jax, jax.numpy as jnp
        import numpy as np
        E = 8
        K = 2
        B, T, d = X.shape
        shared = jax.nn.silu(X @ sW1 + sb1) @ sW2 + sb2
        logits = jnp.einsum('btd,ed->bte', X, routing_W) + expert_bias
        activation = jnp.sqrt(jax.nn.softplus(logits))
        top_vals, top_idx = jax.lax.top_k(activation, K)
        combine = jnp.sum(jax.nn.one_hot(top_idx, E, dtype=X.dtype) * top_vals[..., None], axis=-2)
        Xf = X.reshape(-1, d)
        cf = combine.reshape(-1, E)
        hdn = jax.nn.silu(jnp.einsum('nd,edh->enh', Xf, rW1) + rb1[:, None, :])
        y = jnp.einsum('enh,ehd->end', hdn, rW2) + rb2[:, None, :]
        routed = jnp.einsum('ne,end->nd', cf, y).reshape(B, T, d)
        return shared + routed
    x = x + jnp.tanh(g_xattn[0]) * _L0_xattn_ref(ctx_1024, _layernorm(x, axis=-1))
    x = x + jnp.tanh(g_ffn[0]) * _L0_ffn_ref(_layernorm(x, axis=-1), L0_ffn_routing_W, L0_ffn_expert_bias, L0_ffn_sW1, L0_ffn_sb1, L0_ffn_sW2, L0_ffn_sb2, L0_ffn_rW1, L0_ffn_rb1, L0_ffn_rW2, L0_ffn_rb2)
    return x

_drawn_inputs = setup_inputs


def setup_inputs(seed=0):
    import zlib

    import numpy as np

    out = dict(_drawn_inputs(seed))
    spreads = {'L0_ffn_expert_bias': (0.0, 0.1),
     'L0_ffn_sb1': (0.0, 0.8),
     'L0_ffn_sb2': (0.0, 0.1),
     'L0_ffn_rb1': (0.0, 0.66),
     'L0_ffn_rb2': (0.0, 0.1)}
    factors = {}
    for name, (base, spread) in spreads.items():
        noise = np.random.default_rng([zlib.crc32(name.encode()), seed]).standard_normal(out[name].shape)
        drawn = base * np.exp(spread * noise) if base else spread * noise
        out[name] = jnp.asarray(drawn.astype(out[name].dtype))
    for name, factor in factors.items():
        out[name] = (out[name] * factor).astype(out[name].dtype)
    return out
```

```python
from contextlib import ExitStack

import concourse.bass as bass
from concourse import mybir

ALU = mybir.AluOpType
ACT = mybir.ActivationFunctionType
AX = mybir.AxisListType
F32 = mybir.dt.float32
F16 = mybir.dt.float16
BF16 = mybir.dt.bfloat16
I32 = mybir.dt.int32

P = 128
BIG = 1e30
LN_EPS = 1e-5
QB = 4
RING = 4
CH = 4


def build_kernel(nc, x, ctx_in, g_xattn, g_ffn, routing_W, expert_bias, sW1, sb1, sW2, sb2,
                 rW1, rb1, rW2, rb2, out):
    B, S, DM = x.shape
    E, H = rW1.shape[0], rW1.shape[2]
    NE = E + 1
    KT = DM // P
    NCH = B // CH
    W = S // QB
    LANES = P // (QB * QB)
    T = S + QB
    TOK = CH * S
    assert S == P and B == QB * LANES and H == P and DM == 2 * P and W == 32

    shift = [[(l - LANES * k) % 32 for l in range(32)] for k in range(QB)]
    spread = [[LANES * q + l % LANES for l in range(32)] for q in range(QB)]

    ctx = ExitStack()
    with ctx:
        def sb(name, shape, dt=F32):
            return ctx.enter_context(nc.sbuf_tensor(name, shape, dt))

        def sem(name):
            return ctx.enter_context(nc.semaphore(name))

        xt = sb("xt", [P, B, DM])
        ct = sb("ct", [P, B, DM])
        w1 = sb("w1", [P, KT, NE, H])
        w2 = sb("w2", [P, NE, DM])
        b1row = sb("b1row", [NE, H])
        b1 = sb("b1", [P, NE])
        b2 = sb("b2", [NE, DM])
        rw = sb("rw", [E, DM])
        rwT = sb("rwT", [P, KT, E])
        ebias = sb("ebias", [P, E])
        gates = sb("gates", [P, 2])
        gtanh = sb("gtanh", [P, 2])
        ident = sb("ident", [P, P])
        identb = sb("identb", [P, P], BF16)
        ones = sb("ones", [P, P])
        epst = sb("epst", [P, 1])
        iotaS = sb("iotaS", [P, S])
        iotaL = sb("iotaL", [P, S])
        rank = sb("rank", [P, CH, E])
        sel3 = sb("sel3", [3 * E, E, P], BF16)
        arenaT = sb("arenaT", [P, QB * (T + 1) * W // 2])
        arenaD = sb("arenaD", [P, (W + 1) * T])
        arenaA = sb("arenaA", [P, T * W])
        arenaI = sb("arenaI", [P, T * W])
        arenaF = sb("arenaF", [P, 3 * T * W // 2 + W])
        xnT = arenaT[:, 0:B * DM].rearrange("p (b d) -> p b d", b=B)
        table = arenaT[:, 0:QB * T * W // 2].rearrange("p (q w) -> p q w", q=QB)
        steps = arenaT[:, :].bitcast(F16).rearrange("p (q w) -> p q w", q=QB)
        Dall = arenaD[:, :].rearrange("p (w t) -> p w t", t=T)
        V2 = arenaD[:, :].rearrange("p (t w) -> p t w", w=W + 1)
        Dst = arenaA[:, 0:B * S].rearrange("p (b s) -> p b s", b=B)
        cand = arenaA[:, :]
        iotaJ = arenaI[:, :]
        lowm = arenaI[:, 0:B * S].rearrange("p (b s) -> p b s", b=B)
        FW = T * W // 2
        DL = arenaF[:, 0:FW].bitcast(F16)
        LF = arenaF[:, FW:2 * FW + W].bitcast(F16)
        dV = arenaF[:, 2 * FW + W:3 * FW + W]
        xn = arenaF[:, 0:CH * DM].rearrange("p (k d) -> p k d", k=CH)
        cT = arenaF[:, CH * DM:2 * CH * DM].rearrange("p (k d) -> p k d", k=CH)
        sq = arenaF[:, 2 * CH * DM:3 * CH * DM].rearrange("p (k d) -> p k d", k=CH)
        d2 = arenaF[:, 3 * CH * DM:3 * CH * DM + CH * S].rearrange("p (k s) -> p k s", k=CH)
        scr = arenaF[:, 3 * CH * DM + CH * S:3 * CH * DM + CH * S + DM]
        x2T = arenaA[:, 0:2 * KT * TOK].rearrange("p (r k n) -> p r k n", r=2, k=KT)
        xn2 = arenaD[:, 0:CH * DM].rearrange("p (k d) -> p k d", k=CH)
        hid = arenaD[:, CH * DM:CH * DM + 2 * TOK].rearrange("p (r n) -> p r n", r=2)
        hsc = arenaD[:, CH * DM + 2 * TOK:CH * DM + 4 * TOK].rearrange("p (r n) -> p r n", r=2)
        ot = arenaF[:, 0:CH * DM].rearrange("p (k d) -> p k d", k=CH)
        hsh = arenaD[:, CH * DM + 4 * TOK:CH * DM + 5 * TOK]
        mask = arenaD[:, CH * DM + 5 * TOK:CH * DM + 6 * TOK].rearrange("p (k s) -> p k s", k=CH)
        cf9T = arenaF[0:NE, CH * DM:CH * DM + 2 * TOK].rearrange("p (r n) -> p r n", r=2)
        cf3T = arenaF[0:3 * E, CH * DM + 2 * TOK:CH * DM + 3 * TOK].bitcast(BF16).rearrange("p (r n) -> p r n", r=2)
        st = sb("st", [P, CH, 6])
        mv = sb("mv", [P, CH, 2])
        std = sb("std", [P, CH])
        rstd = sb("rstd", [P, CH])
        bb = sb("bb", [P, B])
        R = [sb(f"R{i}", [P, W + 1]) for i in range(RING)]
        M = [sb(f"M{i}", [P, W + 1]) for i in range(RING)]
        pidx = sb("pidx", [P, 1], I32)
        qidx = sb("qidx", [P, 1], I32)
        qf = sb("qf", [P, 1])
        edgeD = sb("edgeD", [P, 1])
        edgeR = sb("edgeR", [P, 1])
        base = sb("base", [P, 1])
        ends = sb("ends", [P, QB - 1 + T])
        sh = sb("sh", [P, QB - 1, QB - 1 + T])
        VH = sb("VH", [P, S + 1])
        hiC = sb("hiC", [P, B])
        loC = sb("loC", [P, B])
        junk = sb("junk", [P, QB, W])
        var2 = sb("var2", [P, CH])
        neghalf = sb("neghalf", [P, CH])
        half = sb("half", [P, CH * E])
        rstd2 = sb("rstd2", [P, CH])
        lg = sb("lg", [P, CH, E])
        mag = sb("mag", [P, CH, E])
        ex = sb("ex", [P, CH, E])
        ln = sb("ln", [P, CH, E])
        sp = sb("sp", [P, CH, E])
        root = sb("root", [P, CH, E])
        m1 = sb("m1", [P, CH])
        eq = sb("eq", [P, CH, E])
        i1 = sb("i1", [P, CH])
        oh = sb("oh", [P, CH, E])
        oh2 = sb("oh2", [P, CH, E])
        a2 = sb("a2", [P, CH, E])
        cf9 = sb("cf9", [P, CH, NE])
        res = sb("res", [P, CH, E])
        cf3 = sb("cf3", [P, CH, 3 * E], BF16)

        bank = [ctx.enter_context(nc.psum_tensor(f"bank{i}", [P, 512], F32)) for i in range(8)]

        consts = sem("consts")
        x_in = [sem(f"x_in{i}") for i in range(2)]
        c_in = [sem(f"c_in{i}") for i in range(NCH)]
        w_in, passed = sem("w_in"), sem("passed")
        lane_c = sem("lane_c")
        prep_T, prep_c = sem("prep_T"), sem("prep_c")
        dstep = sem("dstep")
        stats, stdd, rst, xn_r, xnT_ps, xnT_r, bb_r, scr_r = (sem(n) for n in (
            "stats", "stdd", "rst", "xn_r", "xnT_ps", "xnT_r", "bb_r", "scr_r"))
        cT_ps, cT_r, sq_r, ab_r, d2_r, dst_r, dall = (sem(n) for n in (
            "cT_ps", "cT_r", "sq_r", "ab_r", "d2_r", "dst_r", "dall"))
        dall_init = sem("dall_init")
        ysh, chain = sem("ysh"), sem("chain")
        flag, mins, costs = sem("flag"), sem("mins"), sem("costs")
        bulk = sem("bulk")
        walk = sem("walk")
        vT, vTc, low_r = sem("vT"), sem("vTc"), sem("low_r")
        mask_r, al, x1_r, st2, mv2, ve, rs2, xn2_r, x2_ps, x2_r = (sem(n) for n in (
            "mask_r", "al", "x1_r", "st2", "mv2", "ve", "rs2", "xn2_r", "x2_ps", "x2_r"))
        lg_ps, lg_r, spa, spb, pw, rt, cfT_ps, cfT_r = (sem(n) for n in (
            "lg_ps", "lg_r", "spa", "spb", "pw", "rt", "cfT_ps", "cfT_r"))
        h_ps, h_r, cb_ps, hs_r, y_e, y_r, o_r, o_out = (sem(n) for n in (
            "h_ps", "h_r", "cb_ps", "hs_r", "y_e", "y_r", "o_r", "o_out"))

        block = ctx.enter_context(nc.Block())

        x_v = x.rearrange("b s d -> s b d")
        c_v = ctx_in.rearrange("b s d -> s b d")
        o_v = out.rearrange("b s d -> s b d")
        N_W = 12

        pT = [bank[k][:, 0:DM] for k in range(CH)]
        pAB = [bank[CH + k][:, 0:S] for k in range(CH)]
        pPrep = bank[3]
        pE = bank[0][:, 0:DM]
        pLg = bank[0][:, DM:DM + CH * E].rearrange("p (k e) -> p k e", e=E)
        pX = [bank[1][:, 0:DM], bank[0][:, 0:DM]]
        pC9 = bank[1][0:NE, :]
        pC3 = bank[0][0:3 * E, 0:TOK // 2].bitcast(BF16)
        pH = [bank[2][:, :], bank[3][:, :]]
        pCb = [bank[4][:, :], bank[7][:, :]]
        pY = [bank[5 + k // 2][:, DM * (k % 2):DM * (k % 2) + DM] for k in range(CH)]

        def col(tile, c, k):
            return tile[:, bass.ds(CH * c + k, 1)] if not isinstance(c, int) else tile[:, CH * c + k:CH * c + k + 1]

        def row(tile, c, k):
            if isinstance(c, int):
                return tile[:, CH * c + k, :]
            return tile[:, bass.ds(CH * c + k, 1), :].rearrange("p a n -> p (a n)")

        def hbuf(par, s):
            return (par + s) % 2

        def schedule(eng, front, ffn):
            for part in front(0, 0):
                part()
            with eng.Fori(0, NCH // 2 - 1) as n:
                ffn(2 * n, 0, front(2 * n + 1, 1))
                ffn(2 * n + 1, 1, front(2 * n + 2, 0))
            ffn(NCH - 2, 0, front(NCH - 1, 1))
            ffn(NCH - 1, 1, [])

        @block.sync
        def _(sync):
            for c in range(NCH):
                if c >= 2:
                    sync.wait_ge(x_in[c % 2], 16 * (c // 2))
                sync.dma_start(xt[:, CH * c:CH * c + CH, :], x_v[:, CH * c:CH * c + CH, :]).then_inc(x_in[c % 2], 16)
            for c in range(NCH):
                sync.dma_start(ct[:, CH * c:CH * c + CH, :], c_v[:, CH * c:CH * c + CH, :]).then_inc(c_in[c], 16)
            sync.wait_ge(dall_init, 2)
            for b in range(B):
                sync.wait_ge(dst_r, b + 1)
                for q in range(QB):
                    lane = 32 * (b // LANES) + LANES * q + b % LANES
                    sync.dma_start(Dall[lane:lane + 1, 1:W + 1, q:q + S],
                                   Dst[W * q:W * q + W, b, :]).then_inc(dall, 16)
            with sync.Fori(0, NCH) as c:
                sync.wait_ge(o_r, CH * c + 2 * CH)
                sync.dma_start(o_v[:, bass.ds(CH * c, CH), :], ot[:, :, :]).then_inc(o_out, 16)
            sync.wait_ge(o_out, 16 * NCH + 16)

        @block.gpsimd
        def _(pool):
            nc.gpsimd.memset(ident[:, :], 0.0).then_inc(lane_c, 1)
            nc.gpsimd.memset(sel3[:, :, :], 0.0).then_inc(lane_c, 1)
            pool.wait_ge(lane_c, 2)
            nc.gpsimd.affine_select(out=ident[:, :], in_=ident[:, :], compare_op=ALU.not_equal, fill=1.0,
                                    base=0, pattern=[[-1, P]], channel_multiplier=1).then_inc(consts, 1)
            nc.gpsimd.memset(ones[:, :], 1.0).then_inc(consts, 1)
            nc.gpsimd.memset(epst[:, :], LN_EPS).then_inc(consts, 1)
            nc.gpsimd.memset(neghalf[:, :], -0.5).then_inc(consts, 1)
            nc.gpsimd.memset(half[:, :], 0.5).then_inc(consts, 1)
            nc.gpsimd.iota(pidx[:, :], pattern=[[0, 1]], base=0, channel_multiplier=1).then_inc(consts, 1)
            pool.dma_start(w1[:, :, E, :], sW1.rearrange("(k p) h -> p k h", p=P)).then_inc(w_in, 16)
            for k in range(KT):
                pool.dma_start(w1[:, k, 0:E, :],
                               rW1[:, P * k:P * k + P, :].rearrange("e p h -> p e h")).then_inc(w_in, 16)
            pool.dma_start(w2[:, E, :], sW2).then_inc(w_in, 16)
            pool.dma_start(w2[:, 0:E, :], rW2.rearrange("e h d -> h e d")).then_inc(w_in, 16)
            pool.dma_start(b1row[0:E, :], rb1).then_inc(w_in, 16)
            pool.dma_start(b1row[E:NE, :], sb1.rearrange("(a h) -> a h", a=1)).then_inc(w_in, 16)
            pool.dma_start(b2[0:E, :], rb2).then_inc(w_in, 16)
            pool.dma_start(b2[E:NE, :], sb2.rearrange("(a h) -> a h", a=1)).then_inc(w_in, 16)
            pool.dma_start(rw[:, :], routing_W).then_inc(w_in, 16)
            pool.dma_start(ebias[:, :],
                           expert_bias.rearrange("(a e) -> a e", a=1).to_broadcast([P, E])).then_inc(w_in, 16)
            pool.dma_start(gates[:, 0:1], g_xattn.rearrange("(a e) -> a e", a=1).to_broadcast([P, 1])).then_inc(w_in, 16)
            pool.dma_start(gates[:, 1:2], g_ffn.rearrange("(a e) -> a e", a=1).to_broadcast([P, 1])).then_inc(w_in, 16)
            nc.gpsimd.iota(iotaS[:, :], pattern=[[1, S]], base=0, channel_multiplier=0,
                           allow_small_or_imprecise_dtypes=True).then_inc(consts, 1)
            nc.gpsimd.iota(rank[:, :, :], pattern=[[0, CH], [-1, E]], base=E, channel_multiplier=0,
                           allow_small_or_imprecise_dtypes=True).then_inc(consts, 1)
            nc.gpsimd.iota(iotaL[:, :], pattern=[[1, S]], base=0, channel_multiplier=0,
                           allow_small_or_imprecise_dtypes=True).then_inc(lane_c, 1)
            nc.gpsimd.iota(iotaJ.rearrange("p (t w) -> p t w", w=W), pattern=[[2 * S, T], [1, W]], base=0,
                           channel_multiplier=0, allow_small_or_imprecise_dtypes=True).then_inc(consts, 1)
            pool.wait_ge(lane_c, 3)
            nc.gpsimd.memset(iotaL[:, 0:1], BIG).then_inc(consts, 1)
            for k in range(3):
                pool.wait_ge(lane_c, 3 + k)
                nc.gpsimd.affine_select(out=sel3[:, :, :], in_=sel3[:, :, :], compare_op=ALU.not_equal, fill=1.0,
                                        base=-E * k, pattern=[[-1, E], [0, P]],
                                        channel_multiplier=1).then_inc(lane_c if k < 2 else consts, 1)
            pool.wait_ge(vTc, 2)
            for c in range(NCH):
                for k in range(CH):
                    nc.gpsimd.tensor_scalar(row(lowm, c, k), iotaS[:, :], col(loC, c, k), None,
                                            ALU.is_lt).then_inc(low_r, 1)
                pool.wait_ge(mv2, CH * c + CH)
                nc.gpsimd.tensor_scalar(var2[:, :], mv[:, :, 1], LN_EPS, None, ALU.add).then_inc(ve, 1)
                pool.wait_ge(ve, c + 1)
                nc.gpsimd.tensor_tensor(rstd2[:, :], var2[:, :], neghalf[:, :], ALU.pow).then_inc(rs2, 1)
                pool.wait_ge(spb, c + 1)
                nc.gpsimd.tensor_tensor(root[:, :, :], sp[:, :, :], half[:, :].rearrange("p (k e) -> p k e", e=E),
                                        ALU.pow).then_inc(pw, 1)

        @block.scalar
        def _(act):
            act.wait_ge(consts, 5)
            with act.Fori(0, NCH) as c:
                act.wait_ge(stats, 2 * CH * c + 2 * CH)
                nc.scalar.activation(std[:, :], mv[:, :, 1], ACT.Sqrt, bias=epst[:, 0:1]).then_inc(stdd, 1)
                for k in range(CH):
                    act.wait_ge(xn_r, CH * c + k + 1)
                    nc.scalar.activation(scr, xn[:, k, :], ACT.Square, accum_out=col(bb, c, k)).then_inc(bb_r, 1)
                    act.wait_ge(xnT_ps, CH * c + k + 1)
                    nc.scalar.mul(row(xnT, c, k), pT[k], -2.0).then_inc(xnT_r, 1)
                    act.wait_ge(bb_r, CH * c + k + 1)
            with act.Fori(0, NCH) as c:
                for k in range(CH):
                    act.wait_ge(cT_r, CH * c + k + 1 + CH)
                    nc.scalar.activation(sq[:, k, :], cT[:, k, :], ACT.Square).then_inc(sq_r, 1)
                for k in range(CH):
                    act.wait_ge(d2_r, CH * c + k + 1 + CH)
                    nc.scalar.activation(row(Dst, c, k), d2[:, k, :], ACT.Sqrt).then_inc(dst_r, 1)

            act.wait_ge(w_in, 16 * 13)
            nc.scalar.activation(gtanh[:, :], gates[:, :], ACT.Tanh).then_inc(prep_c, 1)

            def front(c, par):
                def turn():
                    for k in range(CH):
                        act.wait_ge(x2_ps, CH * c + k + 1)
                        nc.scalar.copy(x2T[:, par, :, S * k:S * k + S],
                                       pX[k % 2].rearrange("p (k n) -> p k n", k=KT)).then_inc(x2_r, 1)

                def softplus():
                    act.wait_ge(lg_r, 2 * c + 2)
                    nc.scalar.activation(ex[:, :, :], mag[:, :, :], ACT.Exp, scale=-1.0).then_inc(spa, 1)
                    act.wait_ge(spa, 2 * c + 1)
                    nc.scalar.activation(ln[:, :, :], ex[:, :, :], ACT.Ln, bias=1.0).then_inc(spa, 1)

                def gates_T():
                    act.wait_ge(cfT_ps, 2 * c + 2)
                    nc.scalar.copy(cf9T[:, par, :], pC9).then_inc(cfT_r, 1)
                    nc.scalar.copy(cf3T[:, par, :], pC3).then_inc(cfT_r, 1)
                return [None, None, None, None, None, turn, softplus, None, None, gates_T]

            def ffn(c, par, parts):
                for s in range(NE):
                    m = E * c + s - 1
                    act.wait_ge(h_ps, NE * c + s + 1)
                    if s == 0:
                        act.wait_ge(ysh, c + 1)
                        nc.scalar.activation(hsh[:, :], pH[hbuf(par, s)], ACT.Silu, bias=b1[:, E:E + 1]).then_inc(h_r, 1)
                    else:
                        act.wait_ge(hs_r, m + 1)
                        nc.scalar.activation(hid[:, (s - 1) % 2, :], pH[hbuf(par, s)], ACT.Silu,
                                             bias=b1[:, s - 1:s]).then_inc(h_r, 1)
                    if parts and parts[s]:
                        parts[s]()
                if parts:
                    parts[NE]()

            act.wait_ge(vTc, 2)
            act.wait_ge(prep_c, 3)
            schedule(act, lambda c, par: [f or (lambda: None) for f in front(c, par)], ffn)

        @block.tensor
        def _(pe):
            pe.wait_ge(consts, 5)
            for c in range(NCH):
                for k in range(CH):
                    pe.wait_ge(xn_r, CH * c + k + 1)
                    pe.wait_ge(xnT_r, CH * c + k + 1)
                    nc.tensor.transpose(pT[k][:, 0:P], xn[:, k, 0:P], ident[:, :])
                    nc.tensor.transpose(pT[k][:, P:DM], xn[:, k, P:DM], ident[:, :]).then_inc(xnT_ps, 1)
            pe.wait_ge(xnT_r, B + CH)
            for c in range(NCH):
                pe.wait_ge(c_in[c], 16)
                for k in range(CH):
                    pe.wait_ge(cT_r, CH * c + k + 1)
                    nc.tensor.transpose(pT[k][:, 0:P], row(ct, c, k)[:, 0:P], ident[:, :])
                    nc.tensor.transpose(pT[k][:, P:DM], row(ct, c, k)[:, P:DM], ident[:, :]).then_inc(cT_ps, 1)
                for k in range(CH):
                    pe.wait_ge(cT_r, CH * c + k + 1 + CH)
                    pe.wait_ge(sq_r, CH * c + k + 1 + CH)
                    pe.wait_ge(d2_r, CH * c + k + 1)
                    for i in range(KT):
                        nc.tensor.matmul(pAB[k], row(xnT, c, k)[:, P * i:P * i + P], cT[:, k, P * i:P * i + P],
                                         start=(i == 0), stop=False)
                    for i in range(KT):
                        mm = nc.tensor.matmul(pAB[k], ones[:, :], sq[:, k, P * i:P * i + P],
                                              start=False, stop=(i == KT - 1))
                    mm.then_inc(ab_r, 1)
            pe.wait_ge(w_in, 16 * 13)
            for k in range(KT):
                nc.tensor.transpose(pPrep[:, E * k:E * k + E], rw[:, P * k:P * k + P], ident[0:E, 0:E])
            nc.tensor.transpose(pPrep[:, 32:32 + NE], b1row[:, :], ident[0:NE, 0:NE]).then_inc(prep_T, 1)
            pe.wait_ge(walk, S + 1)
            nc.tensor.transpose(pPrep[:, 0:P], VH[:, 1:S + 1], ident[:, :])
            nc.tensor.transpose(pPrep[:, P:2 * P], VH[:, 0:S], ident[:, :]).then_inc(vT, 1)

            def front(c, par):
                def align(k):
                    def part():
                        pe.wait_ge(mask_r, CH * c + k + 1)
                        if k == 0:
                            pe.wait_ge(cfT_r, 2 * c + 2)
                        pe.wait_ge(x1_r, CH * c + k + 1)
                        nc.tensor.matmul(pE, mask[:, k, :], row(ct, c, k), start=True, stop=True).then_inc(al, 1)
                    return part

                def turn():
                    pe.wait_ge(cfT_r, 2 * c + 1)
                    for k in range(CH):
                        pe.wait_ge(xn2_r, CH * c + k + 1)
                        pe.wait_ge(x2_r, CH * c + k + 1)
                        nc.tensor.transpose(pX[k % 2][:, 0:P], xn2[:, k, 0:P], ident[:, :])
                        nc.tensor.transpose(pX[k % 2][:, P:DM], xn2[:, k, P:DM], ident[:, :]).then_inc(x2_ps, 1)

                def logits():
                    pe.wait_ge(x2_r, CH * c + CH + 2)
                    for k in range(CH):
                        for i in range(KT):
                            mm = nc.tensor.matmul(pLg[:, k, :], x2T[:, par, i, S * k:S * k + S], rwT[:, i, :],
                                                  start=(i == 0), stop=(i == KT - 1))
                    mm.then_inc(lg_ps, 1)

                def gates_T():
                    pe.wait_ge(rt, 4 * c + 4)
                    for k in range(CH):
                        mm = nc.tensor.transpose(pC9[:, S * k:S * k + S], cf9[:, k, :], ident[:, :])
                    mm.then_inc(cfT_ps, 1)
                    for k in range(CH):
                        mm = nc.tensor.transpose(pC3[:, S * k:S * k + S], cf3[:, k, :], identb[:, :])
                    mm.then_inc(cfT_ps, 1)
                return [align(0), align(1), align(2), align(3), None, turn, logits, None, None, gates_T]

            def ffn(c, par, parts):
                def second(s):
                    if s == 0:
                        pe.wait_ge(h_r, NE * c + s + 3)
                        pe.wait_ge(o_r, CH * c + CH)
                        pe.wait_ge(cfT_r, 2 * c + 3)
                        for k in range(CH):
                            nc.tensor.matmul(pY[k], cf9T[:, par, S * k:S * k + S], b2[:, :],
                                             start=(k % 2 == 0), stop=False, skip_group_check=True)
                    else:
                        pe.wait_ge(hs_r, E * c + s + 2)
                    for k in range(CH):
                        lhs = hsh[:, S * k:S * k + S] if s == 0 else hsc[:, (s - 1) % 2, S * k:S * k + S]
                        mm = nc.tensor.matmul(pY[k], lhs, w2[:, (s - 1) % NE, :], start=False, stop=(s == NE - 1),
                                              skip_group_check=True)
                        if s == NE - 1:
                            mm.then_inc(y_r, 1)
                    if s == 0:
                        mm.then_inc(ysh, 1)
                    elif s < NE - 1:
                        mm.then_inc(y_e, 1)

                for s in range(NE):
                    pe.wait_ge(h_r, NE * c + s + 1)
                    if s == 0:
                        pe.wait_ge(x2_r, CH * c + CH + 2)
                    if s >= 1:
                        if s == 1:
                            pe.wait_ge(cfT_r, 2 * c + 4)
                        pe.wait_ge(hs_r, E * c + s)
                        nc.tensor.matmul(pCb[(s - 1) % 2], sel3[:, s - 1, :], cf3T[:, par, :],
                                         start=True, stop=True).then_inc(cb_ps, 1)
                    for i in range(KT):
                        mm = nc.tensor.matmul(pH[hbuf(par, s)], w1[:, i, (s - 1) % NE, :], x2T[:, par, i, :],
                                              start=(i == 0), stop=(i == KT - 1))
                    mm.then_inc(h_ps, 1)
                    if s >= 1:
                        second(s - 1)
                    if parts and parts[s]:
                        parts[s]()
                second(NE - 1)
                if parts:
                    parts[NE]()

            pe.wait_ge(vTc, 2)
            schedule(pe, lambda c, par: [f or (lambda: None) for f in front(c, par)], ffn)

        @block.vector
        def _(dve):
            def hold():
                dve.sem_inc(passed, 1)

            for s_, n_ in ((xnT_r, CH), (cT_r, CH), (sq_r, CH), (d2_r, CH), (h_r, 2), (hs_r, 2),
                           (ysh, 1), (o_r, CH), (x1_r, 1), (x2_r, 2), (cfT_r, 2), (flag, 4)):
                dve.sem_inc(s_, n_)
            dve.sem_inc(o_out, 16)
            dve.wait_ge(consts, 6)
            nc.vector.tensor_scalar(qidx[:, :], pidx[:, :], 32 - LANES, None, ALU.bitwise_and).then_inc(dstep, 1)
            dve.wait_ge(dstep, 1)
            nc.vector.tensor_copy(qf[:, :], qidx[:, :]).then_inc(dstep, 1)
            dve.wait_ge(dstep, 2)
            nc.vector.tensor_scalar(edgeD[:, :], qf[:, :], 0.0, BIG, ALU.is_equal, ALU.mult).then_inc(dstep, 1)
            nc.vector.tensor_scalar(edgeR[:, :], qf[:, :], 0.0, BIG, ALU.not_equal, ALU.mult).then_inc(dstep, 1)
            nc.vector.tensor_scalar(base[:, :], qf[:, :], (W - 2.0 * S) / LANES, None, ALU.mult).then_inc(dstep, 1)
            nc.vector.memset(arenaD[:, :], BIG).then_inc(dall_init, 1)
            nc.vector.memset(R[RING - 1][:, :], BIG).then_inc(dstep, 1)
            nc.vector.memset(M[RING - 1][:, :], BIG).then_inc(dstep, 1)
            nc.vector.tensor_copy(identb[:, :], ident[:, :]).then_inc(dstep, 1)
            nc.vector.memset(cf9[:, :, :], 1.0).then_inc(dstep, 1)
            nc.vector.memset(VH[:, :], 0.0).then_inc(dstep, 1)
            dve.wait_ge(dstep, 10)
            dve.wait_ge(dall_init, 1)
            nc.vector.tensor_scalar(Dall[:, 0, :], Dall[:, 0, :], 0.0, edgeD[:, 0:1], ALU.mult,
                                    ALU.add).then_inc(dall_init, 1)
            nc.vector.tensor_copy(R[RING - 1][:, 0:1], edgeR[:, :]).then_inc(dstep, 1)
            nc.vector.memset(VH[:, S:S + 1], S - 1.0).then_inc(dstep, 1)
            with dve.Fori(0, NCH // 2) as n:
                for r in range(2):
                    c = 2 * n + r
                    dve.wait_ge(x_in[r], 16 * n + 16)
                    hold()
                    for k in range(CH):
                        nc.vector.bn_stats(st[:, k, :], row(xt, c, k)).then_inc(stats, 1)
                    dve.wait_ge(stats, 2 * CH * c + CH)
                    hold()
                    for k in range(CH):
                        nc.vector.bn_aggr(mv[:, k, :], st[:, k, :]).then_inc(stats, 1)
                    dve.wait_ge(stdd, c + 1)
                    nc.vector.reciprocal(rstd[:, :], std[:, :]).then_inc(rst, 1)
                    dve.wait_ge(rst, c + 1)
                    hold()
                    for k in range(CH):
                        dve.wait_ge(xnT_r, CH * c + k + 1)
                        nc.vector.tensor_scalar(xn[:, k, :], row(xt, c, k), mv[:, k, 0:1], rstd[:, k:k + 1],
                                                ALU.subtract, ALU.mult).then_inc(xn_r, 1)
            dve.wait_ge(bb_r, B)
            with dve.Fori(0, NCH) as c:
                for k in range(CH):
                    dve.wait_ge(cT_ps, CH * c + k + 1)
                    nc.vector.tensor_copy(cT[:, k, :], pT[k]).then_inc(cT_r, 1)
                for k in range(CH):
                    dve.wait_ge(ab_r, CH * c + k + 1)
                    nc.vector.tensor_scalar(d2[:, k, :], pAB[k], col(bb, c, k), 0.0, ALU.add,
                                            ALU.max).then_inc(d2_r, 1)
            dve.wait_ge(prep_T, 1)
            nc.vector.tensor_copy(rwT[:, :, :], pPrep[:, 0:KT * E].rearrange("p (k e) -> p k e", e=E)).then_inc(prep_c, 1)
            nc.vector.tensor_copy(b1[:, :], pPrep[:, 32:32 + NE]).then_inc(prep_c, 1)
            dve.wait_ge(consts, 11)
            nc.vector.tensor_scalar(iotaJ, iotaJ, base[:, 0:1], None, ALU.add).then_inc(dstep, 1)
            dve.wait_ge(dall, 16 * B * QB)
            dve.wait_ge(dstep, 13)
            dve.sem_inc(costs, 1)
            with dve.Fori(0, T // RING) as n:
                for r in range(RING):
                    t = RING * n + r
                    cur, prev = r, (r - 1) % RING
                    dve.wait_ge(flag, 2 * t)
                    dve.wait_ge(costs, t + 1)
                    nc.vector.tensor_tensor(M[cur][:, 1:W + 1], R[prev][:, 1:W + 1], R[prev][:, 0:W],
                                            ALU.min).then_inc(mins, 1)
                    nc.vector.stream_shuffle(M[cur][:, 0:1], R[prev][:, W:W + 1], shift[1]).then_inc(mins, 1)
                    nc.vector.tensor_tensor(DL[:, bass.ds(W * t, W)], R[prev][:, 0:W], R[prev][:, 1:W + 1],
                                            ALU.is_le).then_inc(flag, 1)
                    dve.wait_ge(mins, 2 * t + 2)
                    nc.vector.tensor_tensor_scan(R[cur][:, :], M[cur][:, :],
                                                 Dall[:, :, bass.ds(t, 1)].rearrange("p w a -> p (w a)"),
                                                 BIG, ALU.min, ALU.add).then_inc(costs, 1)
                    nc.vector.tensor_tensor(LF[:, bass.ds(W * t, W)], R[prev][:, 0:W], M[prev][:, 1:W + 1],
                                            ALU.is_lt).then_inc(flag, 1)
            dve.wait_ge(flag, 2 * T + 4)
            nc.vector.memset(LF[:, W * T:W * T + W], 0.0).then_inc(bulk, 1)
            nc.vector.scalar_tensor_tensor(out=cand, in0=DL, scalar=-0.75, in1=iotaJ, op0=ALU.mult,
                                           op1=ALU.add).then_inc(bulk, 1)
            dve.wait_ge(bulk, 2)
            nc.vector.scalar_tensor_tensor(out=cand, in0=LF[:, W:W * T + W], scalar=-1000.0, in1=cand,
                                           op0=ALU.mult, op1=ALU.add).then_inc(bulk, 1)
            dve.wait_ge(bulk, 3)
            nc.vector.tensor_tensor_scan(cand, cand, cand, 0.0, ALU.max, ALU.max).then_inc(bulk, 1)
            nc.vector.memset(ends[:, 0:QB - 1], 0.0).then_inc(bulk, 1)
            dve.wait_ge(bulk, 5)
            candv = cand.rearrange("p (t w) -> p t w", w=W)
            nc.vector.tensor_copy(ends[:, QB - 1:QB - 1 + T], candv[:, :, W - 1]).then_inc(bulk, 1)
            dve.wait_ge(bulk, 6)
            for k in range(1, QB):
                nc.vector.stream_shuffle(sh[:, k - 1, :], ends[:, :], shift[k]).then_inc(bulk, 1)
            dve.wait_ge(bulk, 9)
            nc.vector.tensor_tensor(V2[:, :, 0], sh[:, 0, 2:2 + T], sh[:, 1, 1:1 + T], ALU.max).then_inc(bulk, 1)
            dve.wait_ge(bulk, 10)
            nc.vector.tensor_tensor(V2[:, :, 0], V2[:, :, 0], sh[:, 2, 0:T], ALU.max).then_inc(bulk, 1)
            dve.wait_ge(bulk, 11)
            nc.vector.tensor_tensor(V2[:, :, 1:W + 1], candv, V2[:, :, 0:1].to_broadcast([P, T, W]),
                                    ALU.max).then_inc(bulk, 1)
            dve.wait_ge(bulk, 12)
            nc.vector.tensor_tensor(dV.bitcast(F16)[:, 0:W * T].rearrange("p (t w) -> p t w", w=W),
                                    V2[:, :, 1:W + 1], V2[:, :, 0:W], ALU.subtract).then_inc(bulk, 1)
            dve.wait_ge(bulk, 13)
            for q in range(QB):
                nc.vector.stream_shuffle(table[:, q, :], dV[:, 0:W * T // 2], spread[q]).then_inc(bulk, 1)
            dve.wait_ge(bulk, 13 + QB)
            dve.sem_inc(walk, 1)
            with dve.Fori(0, S - 1) as n:
                dve.wait_ge(walk, n + 1)
                hold()
                skew = steps[:, :, bass.ds(W * (S - 1 - n), W)]
                nc.vector.scalar_tensor_tensor(out=junk[:, :, :], in0=iotaL[:, :].rearrange("p (q w) -> p q w", w=W),
                                               scalar=VH[:, bass.ds(S - n, 1)], in1=skew, op0=ALU.is_le,
                                               op1=ALU.mult, accum_out=VH[:, bass.ds(S - 1 - n, 1)]).then_inc(walk, 1)
            dve.wait_ge(walk, S)
            dve.sem_inc(walk, 1)
            dve.wait_ge(vT, 1)
            for tile, o in ((hiC, 0), (loC, P)):
                nc.vector.tensor_copy(tile[:, :].rearrange("p (g u) -> p g u", g=QB),
                                      pPrep[:, o:o + P].rearrange("p (g u) -> p g u", g=QB)[:, :, 0:LANES]).then_inc(vTc, 1)

            LINKS = 20

            def front(c, par):
                done = [0]

                def link(ins):
                    ins.then_inc(chain, 1)
                    done[0] += 1
                    dve.wait_ge(chain, LINKS * c + done[0])

                def masks(k):
                    dve.wait_ge(low_r, CH * c + k + 1)
                    nc.vector.scalar_tensor_tensor(out=mask[:, k, :], in0=iotaS[:, :], scalar=col(hiC, c, k),
                                                   in1=row(lowm, c, k), op0=ALU.is_le,
                                                   op1=ALU.subtract).then_inc(mask_r, 1)

                def all_masks():
                    for k in range(CH):
                        masks(k)

                def add(k):
                    dve.wait_ge(al, CH * c + k + 1)
                    nc.vector.scalar_tensor_tensor(out=row(xt, c, k), in0=pE, scalar=gtanh[:, 0:1],
                                                   in1=row(xt, c, k), op0=ALU.mult, op1=ALU.add).then_inc(x1_r, 1)
                    dve.wait_ge(x1_r, CH * c + k + 2)
                    hold()
                    nc.vector.bn_stats(st[:, k, :], row(xt, c, k)).then_inc(st2, 1)

                def norm():
                    dve.wait_ge(st2, CH * c + CH)
                    hold()
                    for k in range(CH):
                        nc.vector.bn_aggr(mv[:, k, :], st[:, k, :]).then_inc(mv2, 1)
                    dve.wait_ge(mv2, CH * c + CH)
                    dve.wait_ge(rs2, c + 1)
                    for k in range(CH):
                        nc.vector.tensor_scalar(xn2[:, k, :], row(xt, c, k), mv[:, k, 0:1], rstd2[:, k:k + 1],
                                                ALU.subtract, ALU.mult).then_inc(xn2_r, 1)

                def logit():
                    dve.wait_ge(lg_ps, c + 1)
                    nc.vector.tensor_tensor(lg[:, :, :], pLg, ebias[:, :].unsqueeze(1).to_broadcast([P, CH, E]),
                                            ALU.add).then_inc(lg_r, 1)
                    dve.wait_ge(lg_r, 2 * c + 1)
                    nc.vector.scalar_tensor_tensor(out=mag[:, :, :], in0=lg[:, :, :], scalar=-1.0, in1=lg[:, :, :],
                                                   op0=ALU.mult, op1=ALU.max).then_inc(lg_r, 1)

                def soft():
                    dve.wait_ge(spa, 2 * c + 2)
                    nc.vector.scalar_tensor_tensor(out=sp[:, :, :], in0=lg[:, :, :], scalar=0.0, in1=ln[:, :, :],
                                                   op0=ALU.max, op1=ALU.add).then_inc(spb, 1)

                def top(v, hot, first):
                    link(nc.vector.tensor_reduce(m1[:, :], v[:, :, :], AX.X, ALU.max))
                    link(nc.vector.tensor_tensor(eq[:, :, :], v[:, :, :], m1[:, :].unsqueeze(2).to_broadcast([P, CH, E]),
                                                 ALU.is_equal))
                    link(nc.vector.tensor_tensor(eq[:, :, :], eq[:, :, :], rank[:, :, :], ALU.mult))
                    link(nc.vector.tensor_reduce(i1[:, :], eq[:, :, :], AX.X, ALU.max))
                    link(nc.vector.tensor_tensor(hot[:, :, :], rank[:, :, :],
                                                 i1[:, :].unsqueeze(2).to_broadcast([P, CH, E]), ALU.is_equal))

                def route():
                    dve.wait_ge(pw, c + 1)
                    top(root, oh, True)
                    link(nc.vector.scalar_tensor_tensor(out=a2[:, :, :], in0=oh[:, :, :], scalar=-BIG,
                                                        in1=root[:, :, :], op0=ALU.mult, op1=ALU.add))
                    top(a2, oh2, False)
                    link(nc.vector.tensor_tensor(oh[:, :, :], oh[:, :, :], oh2[:, :, :], ALU.add))
                    cf = cf9[:, :, 0:E]
                    nc.vector.tensor_tensor(cf, oh[:, :, :], root[:, :, :], ALU.mult).then_inc(rt, 1)
                    dve.wait_ge(rt, 4 * c + 1)
                    nc.vector.tensor_copy(cf3[:, :, 0:E], cf).then_inc(rt, 1)
                    dve.wait_ge(rt, 4 * c + 2)
                    link(nc.vector.tensor_tensor(res[:, :, :], cf, cf3[:, :, 0:E], ALU.subtract))
                    nc.vector.tensor_copy(cf3[:, :, E:2 * E], res[:, :, :]).then_inc(rt, 1)
                    dve.wait_ge(rt, 4 * c + 3)
                    link(nc.vector.tensor_tensor(res[:, :, :], res[:, :, :], cf3[:, :, E:2 * E], ALU.subtract))
                    nc.vector.tensor_copy(cf3[:, :, 2 * E:3 * E], res[:, :, :]).then_inc(rt, 1)
                    while done[0] < LINKS:
                        dve.sem_inc(chain, 1)
                        done[0] += 1
                return [all_masks, lambda: add(0), lambda: add(1), lambda: add(2), lambda: (add(3), norm()),
                        None, logit, soft, route, None]

            def ffn(c, par, parts):
                for s in range(NE):
                    if s >= 1:
                        m = E * c + s - 1
                        dve.wait_ge(h_r, NE * c + s + 3)
                        dve.wait_ge(cb_ps, m + 1)
                        if s >= 3:
                            dve.wait_ge(y_e, (E - 1) * c + s - 2)
                        nc.vector.tensor_tensor(hsc[:, (s - 1) % 2, :], hid[:, (s - 1) % 2, :], pCb[(s - 1) % 2],
                                                ALU.mult).then_inc(hs_r, 1)
                    if parts and parts[s]:
                        parts[s]()
                dve.wait_ge(o_out, 16 * c + 16)
                for k in range(CH):
                    dve.wait_ge(y_r, CH * c + k // 2 * 2 + 2)
                    nc.vector.scalar_tensor_tensor(out=ot[:, k, :], in0=pY[k], scalar=gtanh[:, 1:2], in1=row(xt, c, k),
                                                   op0=ALU.mult, op1=ALU.add).then_inc(o_r, 1)

            dve.wait_ge(prep_c, 3)
            schedule(dve, lambda c, par: [f or (lambda: None) for f in front(c, par)], ffn)


_INS = ['x', 'ctx_1024', 'g_xattn', 'g_ffn', 'L0_ffn_routing_W', 'L0_ffn_expert_bias', 'L0_ffn_sW1', 'L0_ffn_sb1',
        'L0_ffn_sW2', 'L0_ffn_sb2', 'L0_ffn_rW1', 'L0_ffn_rb1', 'L0_ffn_rW2', 'L0_ffn_rb2']


def kernel(**inputs):
    import numpy as _np
    import concourse.bacc as _bacc
    from concourse import mybir as _mybir
    from concourse.bass_utils import run_bass_kernel_spmd as _run

    nc = _bacc.Bacc("TRN2", target_bir_lowering=False, num_devices=1)
    arrays, args = {}, []
    for name in _INS:
        a = _np.ascontiguousarray(inputs[name])
        arrays[f"in_{name}"] = a
        args.append(nc.dram_tensor(f"in_{name}", a.shape, _mybir.dt.from_np(a.dtype), kind="ExternalInput").ap())
    o = nc.dram_tensor("out_0", inputs["x"].shape, _mybir.dt.float32, kind="ExternalOutput").ap()
    build_kernel(nc, *args, o)
    r = _run(nc, [arrays], core_ids=[0])
    return r.results[0]["out_0"]
```

```python
from contextlib import ExitStack

import concourse.bass as bass
from concourse import mybir

ALU = mybir.AluOpType
ACT = mybir.ActivationFunctionType
AX = mybir.AxisListType
F32 = mybir.dt.float32
F16 = mybir.dt.float16
BF16 = mybir.dt.bfloat16
I32 = mybir.dt.int32

P = 128
BIG = 1e30
LN_EPS = 1e-5
QB = 4
RING = 4
CH = 4


def build_kernel(nc, x, ctx_in, g_xattn, g_ffn, routing_W, expert_bias, sW1, sb1, sW2, sb2,
                 rW1, rb1, rW2, rb2, out):
    B, S, DM = x.shape
    E, H = rW1.shape[0], rW1.shape[2]
    NE = E + 1
    KT = DM // P
    NCH = B // CH
    W = S // QB
    LANES = P // (QB * QB)
    T = S + QB
    TOK = CH * S
    assert S == P and B == QB * LANES and H == P and DM == 2 * P and W == 32

    shift = [[(l - LANES * k) % 32 for l in range(32)] for k in range(QB)]
    spread = [[LANES * q + l % LANES for l in range(32)] for q in range(QB)]

    ctx = ExitStack()
    with ctx:
        def sb(name, shape, dt=F32):
            return ctx.enter_context(nc.sbuf_tensor(name, shape, dt))

        def sem(name):
            return ctx.enter_context(nc.semaphore(name))

        xt = sb("xt", [P, B, DM])
        ct = sb("ct", [P, B, DM])
        w1 = sb("w1", [P, KT, NE, H])
        w2 = sb("w2", [P, NE, DM])
        b1row = sb("b1row", [NE, H])
        b1 = sb("b1", [P, NE])
        b2 = sb("b2", [NE, DM])
        rw = sb("rw", [E, DM])
        rwT = sb("rwT", [P, KT, E])
        ebias = sb("ebias", [P, E])
        gates = sb("gates", [P, 2])
        gtanh = sb("gtanh", [P, 2])
        ident = sb("ident", [P, P])
        identb = sb("identb", [P, P], BF16)
        ones = sb("ones", [P, P])
        epst = sb("epst", [P, 1])
        iotaS = sb("iotaS", [P, S])
        iotaL = sb("iotaL", [P, S])
        rank = sb("rank", [P, CH, E])
        sel3 = sb("sel3", [3 * E, E, P], BF16)
        arenaT = sb("arenaT", [P, QB * (T + 1) * W // 2])
        arenaD = sb("arenaD", [P, (W + 1) * T])
        arenaA = sb("arenaA", [P, T * W])
        arenaI = sb("arenaI", [P, T * W])
        arenaF = sb("arenaF", [P, 3 * T * W // 2 + W])
        XT = 2 * CH * DM
        xnT = arenaT[:, 0:XT].rearrange("p (r k d) -> p r k d", r=2, k=CH)
        cT = arenaT[:, XT:2 * XT].rearrange("p (r k d) -> p r k d", r=2, k=CH)
        xn = arenaT[:, 2 * XT:2 * XT + CH * DM].rearrange("p (k d) -> p k d", k=CH)
        d2 = arenaT[:, 2 * XT + CH * DM:2 * XT + CH * DM + CH * S].rearrange("p (k s) -> p k s", k=CH)
        sq = arenaF[:, 0:XT].rearrange("p (r k d) -> p r k d", r=2, k=CH)
        table = arenaT[:, 0:QB * T * W // 2].rearrange("p (q w) -> p q w", q=QB)
        steps = arenaT[:, :].bitcast(F16).rearrange("p (q w) -> p q w", q=QB)
        Dall = arenaD[:, :].rearrange("p (w t) -> p w t", t=T)
        V2 = arenaD[:, :].rearrange("p (t w) -> p t w", w=W + 1)
        Dst = arenaA[:, 0:B * S].rearrange("p (b s) -> p b s", b=B)
        cand = arenaA[:, :]
        iotaJ = arenaI[:, :]
        lowm = arenaI[:, 0:B * S].rearrange("p (b s) -> p b s", b=B)
        FW = T * W // 2
        DL = arenaF[:, 0:FW].bitcast(F16)
        LF = arenaF[:, FW:2 * FW + W].bitcast(F16)
        dV = arenaF[:, 2 * FW + W:3 * FW + W]
        x2T = arenaA[:, 0:2 * KT * TOK].rearrange("p (r k n) -> p r k n", r=2, k=KT)
        xn2 = arenaD[:, 0:CH * DM].rearrange("p (k d) -> p k d", k=CH)
        hid = arenaD[:, CH * DM:CH * DM + 2 * TOK].rearrange("p (r n) -> p r n", r=2)
        hsc = arenaD[:, CH * DM + 2 * TOK:CH * DM + 4 * TOK].rearrange("p (r n) -> p r n", r=2)
        ot = arenaF[:, 0:CH * DM].rearrange("p (k d) -> p k d", k=CH)
        hsh = arenaD[:, CH * DM + 4 * TOK:CH * DM + 5 * TOK]
        mask = arenaD[:, CH * DM + 5 * TOK:CH * DM + 6 * TOK].rearrange("p (k s) -> p k s", k=CH)
        cf9T = arenaF[0:NE, CH * DM:CH * DM + 2 * TOK].rearrange("p (r n) -> p r n", r=2)
        cf3T = arenaF[0:3 * E, CH * DM + 2 * TOK:CH * DM + 3 * TOK].bitcast(BF16).rearrange("p (r n) -> p r n", r=2)
        st = sb("st", [P, CH, 6])
        mv = sb("mv", [P, CH, 2])
        bb = sb("bb", [P, 2, CH])
        R = [sb(f"R{i}", [P, W + 1]) for i in range(RING)]
        M = [sb(f"M{i}", [P, W + 1]) for i in range(RING)]
        pidx = sb("pidx", [P, 1], I32)
        qidx = sb("qidx", [P, 1], I32)
        qf = sb("qf", [P, 1])
        edgeD = sb("edgeD", [P, 1])
        edgeR = sb("edgeR", [P, 1])
        base = sb("base", [P, 1])
        ends = sb("ends", [P, QB - 1 + T])
        sh = sb("sh", [P, QB - 1, QB - 1 + T])
        VH = sb("VH", [P, S + 1])
        hiC = sb("hiC", [P, B])
        loC = sb("loC", [P, B])
        junk = sb("junk", [P, QB, W])
        var2 = sb("var2", [P, CH])
        neghalf = sb("neghalf", [P, CH])
        half = sb("half", [P, CH * E])
        rstd2 = sb("rstd2", [P, CH])
        lg = sb("lg", [P, CH, E])
        mag = sb("mag", [P, CH, E])
        ex = sb("ex", [P, CH, E])
        ln = sb("ln", [P, CH, E])
        sp = sb("sp", [P, CH, E])
        root = sb("root", [P, CH, E])
        m1 = sb("m1", [P, CH])
        eq = sb("eq", [P, CH, E])
        i1 = sb("i1", [P, CH])
        oh = sb("oh", [P, CH, E])
        oh2 = sb("oh2", [P, CH, E])
        a2 = sb("a2", [P, CH, E])
        cf9 = sb("cf9", [P, CH, NE])
        res = sb("res", [P, CH, E])
        cf3 = sb("cf3", [P, CH, 3 * E], BF16)

        bank = [ctx.enter_context(nc.psum_tensor(f"bank{i}", [P, 512], F32)) for i in range(8)]

        consts = sem("consts")
        x_in = [sem(f"x_in{i}") for i in range(2)]
        c_in = [sem(f"c_in{i}") for i in range(NCH)]
        w_in, passed = sem("w_in"), sem("passed")
        spilled = [sem(f"spilled{i}") for i in range(NCH)]
        lane_c = sem("lane_c")
        prep_T, prep_c = sem("prep_T"), sem("prep_c")
        dstep = sem("dstep")
        stats, bbs, xn_r, xnT_ps, xnT_r = (sem(n) for n in ("stats", "bbs", "xn_r", "xnT_ps", "xnT_r"))
        cT_ps, cT_r, sq_r, ab_r, d2_r, dst_r, dall = (sem(n) for n in (
            "cT_ps", "cT_r", "sq_r", "ab_r", "d2_r", "dst_r", "dall"))
        dall_init = sem("dall_init")
        ysh, chain = sem("ysh"), sem("chain")
        flag, mins, costs = sem("flag"), sem("mins"), sem("costs")
        bulk = sem("bulk")
        walk = sem("walk")
        vT, vTc, low_r = sem("vT"), sem("vTc"), sem("low_r")
        mask_r, al, x1_r, st2, mv2, ve, rs2, xn2_r, x2_ps, x2_r = (sem(n) for n in (
            "mask_r", "al", "x1_r", "st2", "mv2", "ve", "rs2", "xn2_r", "x2_ps", "x2_r"))
        lg_ps, lg_r, spa, spb, pw, rt, cfT_ps, cfT_r = (sem(n) for n in (
            "lg_ps", "lg_r", "spa", "spb", "pw", "rt", "cfT_ps", "cfT_r"))
        h_ps, h_r, cb_ps, hs_r, y_e, y_r, o_r, o_out = (sem(n) for n in (
            "h_ps", "h_r", "cb_ps", "hs_r", "y_e", "y_r", "o_r", "o_out"))

        dist = nc.dram_tensor("dist", (B, S, S), F32, kind="Internal").ap()

        block = ctx.enter_context(nc.Block())

        x_v = x.rearrange("b s d -> s b d")
        c_v = ctx_in.rearrange("b s d -> s b d")
        o_v = out.rearrange("b s d -> s b d")
        N_W = 12

        pXT = [bank[k][:, 0:DM] for k in range(2)]
        pCT = [bank[2 + k][:, 0:DM] for k in range(2)]
        pAB = [bank[CH + k][:, 0:S] for k in range(CH)]
        pPrep = bank[3]
        pE = bank[0][:, 0:DM]
        pLg = bank[0][:, DM:DM + CH * E].rearrange("p (k e) -> p k e", e=E)
        pX = [bank[1][:, 0:DM], bank[0][:, 0:DM]]
        pC9 = bank[1][0:NE, :]
        pC3 = bank[0][0:3 * E, 0:TOK // 2].bitcast(BF16)
        pH = [bank[2][:, :], bank[3][:, :]]
        pCb = [bank[4][:, :], bank[7][:, :]]
        pY = [bank[5 + k // 2][:, DM * (k % 2):DM * (k % 2) + DM] for k in range(CH)]

        def col(tile, c, k):
            return tile[:, bass.ds(CH * c + k, 1)] if not isinstance(c, int) else tile[:, CH * c + k:CH * c + k + 1]

        def row(tile, c, k):
            if isinstance(c, int):
                return tile[:, CH * c + k, :]
            return tile[:, bass.ds(CH * c + k, 1), :].rearrange("p a n -> p (a n)")

        def hbuf(par, s):
            return (par + s) % 2

        def schedule(eng, front, ffn):
            for part in front(0, 0):
                part()
            with eng.Fori(0, NCH // 2 - 1) as n:
                ffn(2 * n, 0, front(2 * n + 1, 1))
                ffn(2 * n + 1, 1, front(2 * n + 2, 0))
            ffn(NCH - 2, 0, front(NCH - 1, 1))
            ffn(NCH - 1, 1, [])

        def pipeline(eng, first, second):
            first(0, 0)
            with eng.Fori(0, NCH // 2 - 1) as n:
                for r in range(2):
                    first(2 * n + r + 1, 1 - r)
                    second(2 * n + r, r)
            first(NCH - 1, 1)
            second(NCH - 2, 0)
            second(NCH - 1, 1)

        @block.sync
        def _(sync):
            def load(c):
                if c >= 2:
                    sync.wait_ge(x_in[c % 2], 16 * (c // 2))
                sync.dma_start(xt[:, CH * c:CH * c + CH, :], x_v[:, CH * c:CH * c + CH, :]).then_inc(x_in[c % 2], 16)

            def spill(c):
                sync.wait_ge(dst_r, CH * c + 2 * CH)
                sync.dma_start(dist[CH * c:CH * c + CH].rearrange("b w s -> w b s"),
                               Dst[:, CH * c:CH * c + CH, :]).then_inc(spilled[c], 16)

            def fetch(g):
                for c in range(g * LANES // CH, (g + 1) * LANES // CH):
                    sync.wait_ge(spilled[c], 16)
                for q in range(QB):
                    lane = 32 * g + LANES * q
                    sync.dma_start(Dall[lane:lane + LANES, 1:W + 1, q:q + S],
                                   dist[LANES * g:LANES * g + LANES, W * q:W * q + W, :]).then_inc(dall, 16)

            for c in range(4):
                load(c)
            sync.wait_ge(dall_init, 2)
            for c in range(NCH):
                if c + 4 < NCH:
                    load(c + 4)
                spill(c)
                if c % 2:
                    fetch(c // 2)
            with sync.Fori(0, NCH) as c:
                sync.wait_ge(o_r, CH * c + 2 * CH)
                sync.dma_start(o_v[:, bass.ds(CH * c, CH), :], ot[:, :, :]).then_inc(o_out, 16)
            sync.wait_ge(o_out, 16 * NCH + 16)

        @block.gpsimd
        def _(pool):
            nc.gpsimd.memset(ident[:, :], 0.0).then_inc(lane_c, 1)
            nc.gpsimd.memset(sel3[:, :, :], 0.0).then_inc(lane_c, 1)
            pool.wait_ge(lane_c, 2)
            nc.gpsimd.affine_select(out=ident[:, :], in_=ident[:, :], compare_op=ALU.not_equal, fill=1.0,
                                    base=0, pattern=[[-1, P]], channel_multiplier=1).then_inc(consts, 1)
            nc.gpsimd.memset(ones[:, :], 1.0).then_inc(consts, 1)
            nc.gpsimd.memset(epst[:, :], LN_EPS).then_inc(consts, 1)
            nc.gpsimd.memset(neghalf[:, :], -0.5).then_inc(consts, 1)
            nc.gpsimd.memset(half[:, :], 0.5).then_inc(consts, 1)
            nc.gpsimd.iota(pidx[:, :], pattern=[[0, 1]], base=0, channel_multiplier=1).then_inc(consts, 1)
            nc.gpsimd.iota(iotaS[:, :], pattern=[[1, S]], base=0, channel_multiplier=0,
                           allow_small_or_imprecise_dtypes=True).then_inc(consts, 1)
            nc.gpsimd.iota(rank[:, :, :], pattern=[[0, CH], [-1, E]], base=E, channel_multiplier=0,
                           allow_small_or_imprecise_dtypes=True).then_inc(consts, 1)
            nc.gpsimd.iota(iotaL[:, :], pattern=[[1, S]], base=0, channel_multiplier=0,
                           allow_small_or_imprecise_dtypes=True).then_inc(lane_c, 1)
            nc.gpsimd.iota(iotaJ.rearrange("p (t w) -> p t w", w=W), pattern=[[2 * S, T], [1, W]], base=0,
                           channel_multiplier=0, allow_small_or_imprecise_dtypes=True).then_inc(consts, 1)
            pool.wait_ge(lane_c, 3)
            nc.gpsimd.memset(iotaL[:, 0:1], BIG).then_inc(consts, 1)
            for k in range(3):
                pool.wait_ge(lane_c, 3 + k)
                nc.gpsimd.affine_select(out=sel3[:, :, :], in_=sel3[:, :, :], compare_op=ALU.not_equal, fill=1.0,
                                        base=-E * k, pattern=[[-1, E], [0, P]],
                                        channel_multiplier=1).then_inc(lane_c if k < 2 else consts, 1)
            def root_of(c):
                pool.wait_ge(stats, 2 * CH * c + 2 * CH)
                nc.gpsimd.tensor_scalar(var2[:, :], mv[:, :, 1], LN_EPS, None, ALU.add).then_inc(ve, 1)
                pool.wait_ge(ve, c + 1)
                nc.gpsimd.tensor_tensor(rstd2[:, :], var2[:, :], neghalf[:, :], ALU.pow).then_inc(rs2, 1)

            def squares(c):
                for k in range(CH):
                    pool.wait_ge(cT_r, CH * c + k + 1 + 2)
                    nc.gpsimd.tensor_tensor(sq[:, c % 2, k, :], cT[:, c % 2, k, :], cT[:, c % 2, k, :],
                                            ALU.mult).then_inc(sq_r, 1)

            root_of(0)
            for c in range(NCH):
                if c + 1 < NCH:
                    root_of(c + 1)
                squares(c)
            pool.dma_start(w1[:, :, E, :], sW1.rearrange("(k p) h -> p k h", p=P)).then_inc(w_in, 16)
            for k in range(KT):
                pool.dma_start(w1[:, k, 0:E, :],
                               rW1[:, P * k:P * k + P, :].rearrange("e p h -> p e h")).then_inc(w_in, 16)
            pool.dma_start(w2[:, E, :], sW2).then_inc(w_in, 16)
            pool.dma_start(w2[:, 0:E, :], rW2.rearrange("e h d -> h e d")).then_inc(w_in, 16)
            pool.dma_start(b1row[0:E, :], rb1).then_inc(w_in, 16)
            pool.dma_start(b1row[E:NE, :], sb1.rearrange("(a h) -> a h", a=1)).then_inc(w_in, 16)
            pool.dma_start(b2[0:E, :], rb2).then_inc(w_in, 16)
            pool.dma_start(b2[E:NE, :], sb2.rearrange("(a h) -> a h", a=1)).then_inc(w_in, 16)
            pool.dma_start(rw[:, :], routing_W).then_inc(w_in, 16)
            pool.dma_start(ebias[:, :],
                           expert_bias.rearrange("(a e) -> a e", a=1).to_broadcast([P, E])).then_inc(w_in, 16)
            pool.dma_start(gates[:, 0:1], g_xattn.rearrange("(a e) -> a e", a=1).to_broadcast([P, 1])).then_inc(w_in, 16)
            pool.dma_start(gates[:, 1:2], g_ffn.rearrange("(a e) -> a e", a=1).to_broadcast([P, 1])).then_inc(w_in, 16)
            pool.wait_ge(vTc, 2)
            for c in range(NCH):
                for k in range(CH):
                    nc.gpsimd.tensor_scalar(row(lowm, c, k), iotaS[:, :], col(loC, c, k), None,
                                            ALU.is_lt).then_inc(low_r, 1)
                pool.wait_ge(mv2, CH * c + CH)
                nc.gpsimd.tensor_scalar(var2[:, :], mv[:, :, 1], LN_EPS, None, ALU.add).then_inc(ve, 1)
                pool.wait_ge(ve, NCH + c + 1)
                nc.gpsimd.tensor_tensor(rstd2[:, :], var2[:, :], neghalf[:, :], ALU.pow).then_inc(rs2, 1)
                pool.wait_ge(spb, c + 1)
                nc.gpsimd.tensor_tensor(root[:, :, :], sp[:, :, :], half[:, :].rearrange("p (k e) -> p k e", e=E),
                                        ALU.pow).then_inc(pw, 1)

        @block.scalar
        def _(act):
            for c in range(NCH):
                act.dma_start(ct[:, CH * c:CH * c + CH, :], c_v[:, CH * c:CH * c + CH, :]).then_inc(c_in[c], 16)
            nc.scalar.preload_act_table_set("sqrt_and_others")

            def evacuate(c, par):
                for k in range(CH):
                    act.wait_ge(xnT_ps, CH * c + k + 1)
                    nc.scalar.mul(xnT[:, par, k, :], pXT[k % 2], -2.0).then_inc(xnT_r, 1)
                    act.wait_ge(cT_ps, CH * c + k + 1)
                    nc.scalar.copy(cT[:, par, k, :], pCT[k % 2]).then_inc(cT_r, 1)

            def roots(c, par):
                for k in range(CH):
                    act.wait_ge(d2_r, CH * c + k + 1 + CH)
                    nc.scalar.activation(row(Dst, c, k), d2[:, k, :], ACT.Sqrt).then_inc(dst_r, 1)

            pipeline(act, evacuate, roots)
            nc.scalar.preload_act_table_set("silu_and_others")
            act.wait_ge(w_in, 16 * 13)
            nc.scalar.activation(gtanh[:, :], gates[:, :], ACT.Tanh).then_inc(prep_c, 1)

            def front(c, par):
                def turn():
                    for k in range(CH):
                        act.wait_ge(x2_ps, CH * c + k + 1)
                        nc.scalar.copy(x2T[:, par, :, S * k:S * k + S],
                                       pX[k % 2].rearrange("p (k n) -> p k n", k=KT)).then_inc(x2_r, 1)

                def softplus():
                    act.wait_ge(lg_r, 2 * c + 2)
                    nc.scalar.activation(ex[:, :, :], mag[:, :, :], ACT.Exp, scale=-1.0).then_inc(spa, 1)
                    act.wait_ge(spa, 2 * c + 1)
                    nc.scalar.activation(ln[:, :, :], ex[:, :, :], ACT.Ln, bias=1.0).then_inc(spa, 1)

                def gates_T():
                    act.wait_ge(cfT_ps, 2 * c + 2)
                    nc.scalar.copy(cf9T[:, par, :], pC9).then_inc(cfT_r, 1)
                    nc.scalar.copy(cf3T[:, par, :], pC3).then_inc(cfT_r, 1)
                return [None, None, None, None, None, turn, softplus, None, None, gates_T]

            def ffn(c, par, parts):
                for s in range(NE):
                    m = E * c + s - 1
                    act.wait_ge(h_ps, NE * c + s + 1)
                    if s == 0:
                        act.wait_ge(ysh, c + 1)
                        nc.scalar.activation(hsh[:, :], pH[hbuf(par, s)], ACT.Silu, bias=b1[:, E:E + 1]).then_inc(h_r, 1)
                    else:
                        act.wait_ge(hs_r, m + 1)
                        nc.scalar.activation(hid[:, (s - 1) % 2, :], pH[hbuf(par, s)], ACT.Silu,
                                             bias=b1[:, s - 1:s]).then_inc(h_r, 1)
                    if parts and parts[s]:
                        parts[s]()
                if parts:
                    parts[NE]()

            act.wait_ge(vTc, 2)
            act.wait_ge(prep_c, 3)
            schedule(act, lambda c, par: [f or (lambda: None) for f in front(c, par)], ffn)

        @block.tensor
        def _(pe):
            pe.wait_ge(consts, 5)
            def turn_chunk(c):
                pe.wait_ge(c_in[c], 16)
                for k in range(CH):
                    pe.wait_ge(xn_r, CH * c + k + 1)
                    pe.wait_ge(xnT_r, CH * c + k + 1)
                    nc.tensor.transpose(pXT[k % 2][:, 0:P], xn[:, k, 0:P], ident[:, :])
                    nc.tensor.transpose(pXT[k % 2][:, P:DM], xn[:, k, P:DM], ident[:, :]).then_inc(xnT_ps, 1)
                    pe.wait_ge(cT_r, CH * c + k + 1)
                    nc.tensor.transpose(pCT[k % 2][:, 0:P], row(ct, c, k)[:, 0:P], ident[:, :])
                    nc.tensor.transpose(pCT[k % 2][:, P:DM], row(ct, c, k)[:, P:DM], ident[:, :]).then_inc(cT_ps, 1)

            def square_distances(c):
                for k in range(CH):
                    pe.wait_ge(xnT_r, CH * c + k + 1 + 2)
                    pe.wait_ge(cT_r, CH * c + k + 1 + 2)
                    pe.wait_ge(d2_r, CH * c + k + 1)
                    for i in range(KT):
                        nc.tensor.matmul(pAB[k], xnT[:, c % 2, k, P * i:P * i + P], cT[:, c % 2, k, P * i:P * i + P],
                                         start=(i == 0), stop=False)
                    pe.wait_ge(sq_r, CH * c + k + 1)
                    for i in range(KT):
                        mm = nc.tensor.matmul(pAB[k], ones[:, :], sq[:, c % 2, k, P * i:P * i + P],
                                              start=False, stop=(i == KT - 1))
                    mm.then_inc(ab_r, 1)

            turn_chunk(0)
            for c in range(NCH):
                if c + 1 < NCH:
                    turn_chunk(c + 1)
                square_distances(c)
            pe.wait_ge(w_in, 16 * 13)
            for k in range(KT):
                nc.tensor.transpose(pPrep[:, E * k:E * k + E], rw[:, P * k:P * k + P], ident[0:E, 0:E])
            nc.tensor.transpose(pPrep[:, 32:32 + NE], b1row[:, :], ident[0:NE, 0:NE]).then_inc(prep_T, 1)
            pe.wait_ge(walk, S + 1)
            nc.tensor.transpose(pPrep[:, 0:P], VH[:, 1:S + 1], ident[:, :])
            nc.tensor.transpose(pPrep[:, P:2 * P], VH[:, 0:S], ident[:, :]).then_inc(vT, 1)

            def front(c, par):
                def align(k):
                    def part():
                        pe.wait_ge(mask_r, CH * c + k + 1)
                        if k == 0:
                            pe.wait_ge(cfT_r, 2 * c + 2)
                        pe.wait_ge(x1_r, CH * c + k + 1)
                        nc.tensor.matmul(pE, mask[:, k, :], row(ct, c, k), start=True, stop=True).then_inc(al, 1)
                    return part

                def turn():
                    pe.wait_ge(cfT_r, 2 * c + 1)
                    for k in range(CH):
                        pe.wait_ge(xn2_r, CH * c + k + 1)
                        pe.wait_ge(x2_r, CH * c + k + 1)
                        nc.tensor.transpose(pX[k % 2][:, 0:P], xn2[:, k, 0:P], ident[:, :])
                        nc.tensor.transpose(pX[k % 2][:, P:DM], xn2[:, k, P:DM], ident[:, :]).then_inc(x2_ps, 1)

                def logits():
                    pe.wait_ge(x2_r, CH * c + CH + 2)
                    for k in range(CH):
                        for i in range(KT):
                            mm = nc.tensor.matmul(pLg[:, k, :], x2T[:, par, i, S * k:S * k + S], rwT[:, i, :],
                                                  start=(i == 0), stop=(i == KT - 1))
                    mm.then_inc(lg_ps, 1)

                def gates_T():
                    pe.wait_ge(rt, 4 * c + 4)
                    for k in range(CH):
                        mm = nc.tensor.transpose(pC9[:, S * k:S * k + S], cf9[:, k, :], ident[:, :])
                    mm.then_inc(cfT_ps, 1)
                    for k in range(CH):
                        mm = nc.tensor.transpose(pC3[:, S * k:S * k + S], cf3[:, k, :], identb[:, :])
                    mm.then_inc(cfT_ps, 1)
                return [align(0), align(1), align(2), align(3), None, turn, logits, None, None, gates_T]

            def ffn(c, par, parts):
                def second(s):
                    if s == 0:
                        pe.wait_ge(h_r, NE * c + s + 3)
                        pe.wait_ge(o_r, CH * c + CH)
                        pe.wait_ge(cfT_r, 2 * c + 3)
                        for k in range(CH):
                            nc.tensor.matmul(pY[k], cf9T[:, par, S * k:S * k + S], b2[:, :],
                                             start=(k % 2 == 0), stop=False, skip_group_check=True)
                    else:
                        pe.wait_ge(hs_r, E * c + s + 2)
                    for k in range(CH):
                        lhs = hsh[:, S * k:S * k + S] if s == 0 else hsc[:, (s - 1) % 2, S * k:S * k + S]
                        mm = nc.tensor.matmul(pY[k], lhs, w2[:, (s - 1) % NE, :], start=False, stop=(s == NE - 1),
                                              skip_group_check=True)
                        if s == NE - 1:
                            mm.then_inc(y_r, 1)
                    if s == 0:
                        mm.then_inc(ysh, 1)
                    elif s < NE - 1:
                        mm.then_inc(y_e, 1)

                for s in range(NE):
                    pe.wait_ge(h_r, NE * c + s + 1)
                    if s == 0:
                        pe.wait_ge(x2_r, CH * c + CH + 2)
                    if s >= 1:
                        if s == 1:
                            pe.wait_ge(cfT_r, 2 * c + 4)
                        pe.wait_ge(hs_r, E * c + s)
                        nc.tensor.matmul(pCb[(s - 1) % 2], sel3[:, s - 1, :], cf3T[:, par, :],
                                         start=True, stop=True).then_inc(cb_ps, 1)
                    for i in range(KT):
                        mm = nc.tensor.matmul(pH[hbuf(par, s)], w1[:, i, (s - 1) % NE, :], x2T[:, par, i, :],
                                              start=(i == 0), stop=(i == KT - 1))
                    mm.then_inc(h_ps, 1)
                    if s >= 1:
                        second(s - 1)
                    if parts and parts[s]:
                        parts[s]()
                second(NE - 1)
                if parts:
                    parts[NE]()

            pe.wait_ge(vTc, 2)
            schedule(pe, lambda c, par: [f or (lambda: None) for f in front(c, par)], ffn)

        @block.vector
        def _(dve):
            def hold():
                dve.sem_inc(passed, 1)

            for s_, n_ in ((xnT_r, 2), (cT_r, 2), (dst_r, CH), (d2_r, CH), (h_r, 2), (hs_r, 2),
                           (ysh, 1), (o_r, CH), (x1_r, 1), (x2_r, 2), (cfT_r, 2), (flag, 4)):
                dve.sem_inc(s_, n_)
            dve.sem_inc(o_out, 16)
            dve.wait_ge(consts, 6)
            nc.vector.tensor_scalar(qidx[:, :], pidx[:, :], 32 - LANES, None, ALU.bitwise_and).then_inc(dstep, 1)
            dve.wait_ge(dstep, 1)
            nc.vector.tensor_copy(qf[:, :], qidx[:, :]).then_inc(dstep, 1)
            dve.wait_ge(dstep, 2)
            nc.vector.tensor_scalar(edgeD[:, :], qf[:, :], 0.0, BIG, ALU.is_equal, ALU.mult).then_inc(dstep, 1)
            nc.vector.tensor_scalar(edgeR[:, :], qf[:, :], 0.0, BIG, ALU.not_equal, ALU.mult).then_inc(dstep, 1)
            nc.vector.tensor_scalar(base[:, :], qf[:, :], (W - 2.0 * S) / LANES, None, ALU.mult).then_inc(dstep, 1)
            nc.vector.memset(arenaD[:, :], BIG).then_inc(dall_init, 1)
            nc.vector.memset(R[RING - 1][:, :], BIG).then_inc(dstep, 1)
            nc.vector.memset(M[RING - 1][:, :], BIG).then_inc(dstep, 1)
            nc.vector.tensor_copy(identb[:, :], ident[:, :]).then_inc(dstep, 1)
            nc.vector.memset(cf9[:, :, :], 1.0).then_inc(dstep, 1)
            nc.vector.memset(VH[:, :], 0.0).then_inc(dstep, 1)
            dve.wait_ge(dstep, 10)
            dve.wait_ge(dall_init, 1)
            nc.vector.tensor_scalar(Dall[:, 0, :], Dall[:, 0, :], 0.0, edgeD[:, 0:1], ALU.mult,
                                    ALU.add).then_inc(dall_init, 1)
            nc.vector.tensor_copy(R[RING - 1][:, 0:1], edgeR[:, :]).then_inc(dstep, 1)
            nc.vector.memset(VH[:, S:S + 1], S - 1.0).then_inc(dstep, 1)
            def normalise(c, par):
                dve.wait_ge(x_in[par], 8 * (c - par) + 16)
                hold()
                for k in range(CH):
                    nc.vector.bn_stats(st[:, k, :], row(xt, c, k)).then_inc(stats, 1)
                dve.wait_ge(stats, 2 * CH * c + CH)
                hold()
                for k in range(CH):
                    nc.vector.bn_aggr(mv[:, k, :], st[:, k, :]).then_inc(stats, 1)
                dve.wait_ge(rs2, c + 1)
                hold()
                for k in range(CH):
                    if not (isinstance(c, int) and CH * c + k < 2):
                        dve.wait_ge(xnT_r, CH * c + k - 1)
                    nc.vector.tensor_scalar(xn[:, k, :], row(xt, c, k), mv[:, k, 0:1], rstd2[:, k:k + 1],
                                            ALU.subtract, ALU.mult).then_inc(xn_r, 1)
                nc.vector.scalar_tensor_tensor(out=bb[:, par, :], in0=mv[:, :, 1], scalar=float(DM), in1=rstd2[:, :],
                                               op0=ALU.mult, op1=ALU.mult).then_inc(bbs, 1)
                dve.wait_ge(bbs, 2 * c + 1)
                nc.vector.tensor_tensor(bb[:, par, :], bb[:, par, :], rstd2[:, :], ALU.mult).then_inc(bbs, 1)

            def guard(c, par):
                dve.wait_ge(bbs, 2 * c + 2)
                for k in range(CH):
                    dve.wait_ge(ab_r, CH * c + k + 1)
                    dve.wait_ge(dst_r, CH * c + k + 1)
                    nc.vector.tensor_scalar(d2[:, k, :], pAB[k], bb[:, par, k:k + 1], 0.0, ALU.add,
                                            ALU.max).then_inc(d2_r, 1)

            pipeline(dve, normalise, guard)
            dve.wait_ge(prep_T, 1)
            nc.vector.tensor_copy(rwT[:, :, :], pPrep[:, 0:KT * E].rearrange("p (k e) -> p k e", e=E)).then_inc(prep_c, 1)
            nc.vector.tensor_copy(b1[:, :], pPrep[:, 32:32 + NE]).then_inc(prep_c, 1)
            dve.wait_ge(consts, 11)
            nc.vector.tensor_scalar(iotaJ, iotaJ, base[:, 0:1], None, ALU.add).then_inc(dstep, 1)
            dve.wait_ge(dall, 16 * QB * QB)
            dve.wait_ge(dstep, 13)
            dve.sem_inc(costs, 1)
            for t in range(T):
                cur, prev = t % RING, (t - 1) % RING
                dve.wait_ge(flag, 2 * t)
                dve.wait_ge(costs, t + 1)
                nc.vector.tensor_tensor(M[cur][:, 1:W + 1], R[prev][:, 1:W + 1], R[prev][:, 0:W],
                                        ALU.min).then_inc(mins, 1)
                nc.vector.stream_shuffle(M[cur][:, 0:1], R[prev][:, W:W + 1], shift[1]).then_inc(mins, 1)
                nc.vector.tensor_tensor(DL[:, W * t:W * t + W], R[prev][:, 0:W], R[prev][:, 1:W + 1],
                                        ALU.is_le).then_inc(flag, 1)
                dve.wait_ge(mins, 2 * t + 2)
                nc.vector.tensor_tensor_scan(R[cur][:, :], M[cur][:, :], Dall[:, :, t], BIG, ALU.min,
                                             ALU.add).then_inc(costs, 1)
                nc.vector.tensor_tensor(LF[:, W * t:W * t + W], R[prev][:, 0:W], M[prev][:, 1:W + 1],
                                        ALU.is_lt).then_inc(flag, 1)
            dve.wait_ge(flag, 2 * T + 4)
            nc.vector.memset(LF[:, W * T:W * T + W], 0.0).then_inc(bulk, 1)
            nc.vector.scalar_tensor_tensor(out=cand, in0=DL, scalar=-0.75, in1=iotaJ, op0=ALU.mult,
                                           op1=ALU.add).then_inc(bulk, 1)
            dve.wait_ge(bulk, 2)
            nc.vector.scalar_tensor_tensor(out=cand, in0=LF[:, W:W * T + W], scalar=-1000.0, in1=cand,
                                           op0=ALU.mult, op1=ALU.add).then_inc(bulk, 1)
            dve.wait_ge(bulk, 3)
            nc.vector.tensor_tensor_scan(cand, cand, cand, 0.0, ALU.max, ALU.max).then_inc(bulk, 1)
            nc.vector.memset(ends[:, 0:QB - 1], 0.0).then_inc(bulk, 1)
            dve.wait_ge(bulk, 5)
            candv = cand.rearrange("p (t w) -> p t w", w=W)
            nc.vector.tensor_copy(ends[:, QB - 1:QB - 1 + T], candv[:, :, W - 1]).then_inc(bulk, 1)
            dve.wait_ge(bulk, 6)
            for k in range(1, QB):
                nc.vector.stream_shuffle(sh[:, k - 1, :], ends[:, :], shift[k]).then_inc(bulk, 1)
            dve.wait_ge(bulk, 9)
            nc.vector.tensor_tensor(V2[:, :, 0], sh[:, 0, 2:2 + T], sh[:, 1, 1:1 + T], ALU.max).then_inc(bulk, 1)
            dve.wait_ge(bulk, 10)
            nc.vector.tensor_tensor(V2[:, :, 0], V2[:, :, 0], sh[:, 2, 0:T], ALU.max).then_inc(bulk, 1)
            dve.wait_ge(bulk, 11)
            nc.vector.tensor_tensor(V2[:, :, 1:W + 1], candv, V2[:, :, 0:1].to_broadcast([P, T, W]),
                                    ALU.max).then_inc(bulk, 1)
            dve.wait_ge(bulk, 12)
            nc.vector.tensor_tensor(dV.bitcast(F16)[:, 0:W * T].rearrange("p (t w) -> p t w", w=W),
                                    V2[:, :, 1:W + 1], V2[:, :, 0:W], ALU.subtract).then_inc(bulk, 1)
            dve.wait_ge(bulk, 13)
            for q in range(QB):
                nc.vector.stream_shuffle(table[:, q, :], dV[:, 0:W * T // 2], spread[q]).then_inc(bulk, 1)
            dve.wait_ge(bulk, 13 + QB)
            dve.sem_inc(walk, 1)
            for i in range(S - 1, 0, -1):
                dve.wait_ge(walk, S - i)
                nc.vector.scalar_tensor_tensor(out=junk[:, :, :], in0=iotaL[:, :].rearrange("p (q w) -> p q w", w=W),
                                               scalar=VH[:, i + 1:i + 2], in1=steps[:, :, W * i:W * i + W],
                                               op0=ALU.is_le, op1=ALU.mult, accum_out=VH[:, i:i + 1]).then_inc(walk, 1)
            dve.wait_ge(walk, S)
            dve.sem_inc(walk, 1)
            dve.wait_ge(vT, 1)
            for tile, o in ((hiC, 0), (loC, P)):
                nc.vector.tensor_copy(tile[:, :].rearrange("p (g u) -> p g u", g=QB),
                                      pPrep[:, o:o + P].rearrange("p (g u) -> p g u", g=QB)[:, :, 0:LANES]).then_inc(vTc, 1)

            LINKS = 20

            def front(c, par):
                done = [0]

                def link(ins):
                    ins.then_inc(chain, 1)
                    done[0] += 1
                    dve.wait_ge(chain, LINKS * c + done[0])

                def masks(k):
                    dve.wait_ge(low_r, CH * c + k + 1)
                    nc.vector.scalar_tensor_tensor(out=mask[:, k, :], in0=iotaS[:, :], scalar=col(hiC, c, k),
                                                   in1=row(lowm, c, k), op0=ALU.is_le,
                                                   op1=ALU.subtract).then_inc(mask_r, 1)

                def all_masks():
                    for k in range(CH):
                        masks(k)

                def add(k):
                    dve.wait_ge(al, CH * c + k + 1)
                    nc.vector.scalar_tensor_tensor(out=row(xt, c, k), in0=pE, scalar=gtanh[:, 0:1],
                                                   in1=row(xt, c, k), op0=ALU.mult, op1=ALU.add).then_inc(x1_r, 1)
                    dve.wait_ge(x1_r, CH * c + k + 2)
                    hold()
                    nc.vector.bn_stats(st[:, k, :], row(xt, c, k)).then_inc(st2, 1)

                def norm():
                    dve.wait_ge(st2, CH * c + CH)
                    hold()
                    for k in range(CH):
                        nc.vector.bn_aggr(mv[:, k, :], st[:, k, :]).then_inc(mv2, 1)
                    dve.wait_ge(mv2, CH * c + CH)
                    dve.wait_ge(rs2, NCH + c + 1)
                    for k in range(CH):
                        nc.vector.tensor_scalar(xn2[:, k, :], row(xt, c, k), mv[:, k, 0:1], rstd2[:, k:k + 1],
                                                ALU.subtract, ALU.mult).then_inc(xn2_r, 1)

                def logit():
                    dve.wait_ge(lg_ps, c + 1)
                    nc.vector.tensor_tensor(lg[:, :, :], pLg, ebias[:, :].unsqueeze(1).to_broadcast([P, CH, E]),
                                            ALU.add).then_inc(lg_r, 1)
                    dve.wait_ge(lg_r, 2 * c + 1)
                    nc.vector.scalar_tensor_tensor(out=mag[:, :, :], in0=lg[:, :, :], scalar=-1.0, in1=lg[:, :, :],
                                                   op0=ALU.mult, op1=ALU.max).then_inc(lg_r, 1)

                def soft():
                    dve.wait_ge(spa, 2 * c + 2)
                    nc.vector.scalar_tensor_tensor(out=sp[:, :, :], in0=lg[:, :, :], scalar=0.0, in1=ln[:, :, :],
                                                   op0=ALU.max, op1=ALU.add).then_inc(spb, 1)

                def top(v, hot, first):
                    link(nc.vector.tensor_reduce(m1[:, :], v[:, :, :], AX.X, ALU.max))
                    link(nc.vector.tensor_tensor(eq[:, :, :], v[:, :, :], m1[:, :].unsqueeze(2).to_broadcast([P, CH, E]),
                                                 ALU.is_equal))
                    link(nc.vector.tensor_tensor(eq[:, :, :], eq[:, :, :], rank[:, :, :], ALU.mult))
                    link(nc.vector.tensor_reduce(i1[:, :], eq[:, :, :], AX.X, ALU.max))
                    link(nc.vector.tensor_tensor(hot[:, :, :], rank[:, :, :],
                                                 i1[:, :].unsqueeze(2).to_broadcast([P, CH, E]), ALU.is_equal))

                def route():
                    dve.wait_ge(pw, c + 1)
                    top(root, oh, True)
                    link(nc.vector.scalar_tensor_tensor(out=a2[:, :, :], in0=oh[:, :, :], scalar=-BIG,
                                                        in1=root[:, :, :], op0=ALU.mult, op1=ALU.add))
                    top(a2, oh2, False)
                    link(nc.vector.tensor_tensor(oh[:, :, :], oh[:, :, :], oh2[:, :, :], ALU.add))
                    cf = cf9[:, :, 0:E]
                    nc.vector.tensor_tensor(cf, oh[:, :, :], root[:, :, :], ALU.mult).then_inc(rt, 1)
                    dve.wait_ge(rt, 4 * c + 1)
                    nc.vector.tensor_copy(cf3[:, :, 0:E], cf).then_inc(rt, 1)
                    dve.wait_ge(rt, 4 * c + 2)
                    link(nc.vector.tensor_tensor(res[:, :, :], cf, cf3[:, :, 0:E], ALU.subtract))
                    nc.vector.tensor_copy(cf3[:, :, E:2 * E], res[:, :, :]).then_inc(rt, 1)
                    dve.wait_ge(rt, 4 * c + 3)
                    link(nc.vector.tensor_tensor(res[:, :, :], res[:, :, :], cf3[:, :, E:2 * E], ALU.subtract))
                    nc.vector.tensor_copy(cf3[:, :, 2 * E:3 * E], res[:, :, :]).then_inc(rt, 1)
                    while done[0] < LINKS:
                        dve.sem_inc(chain, 1)
                        done[0] += 1
                return [all_masks, lambda: add(0), lambda: add(1), lambda: add(2), lambda: (add(3), norm()),
                        None, logit, soft, route, None]

            def ffn(c, par, parts):
                for s in range(NE):
                    if s >= 1:
                        m = E * c + s - 1
                        dve.wait_ge(h_r, NE * c + s + 3)
                        dve.wait_ge(cb_ps, m + 1)
                        if s >= 3:
                            dve.wait_ge(y_e, (E - 1) * c + s - 2)
                        nc.vector.tensor_tensor(hsc[:, (s - 1) % 2, :], hid[:, (s - 1) % 2, :], pCb[(s - 1) % 2],
                                                ALU.mult).then_inc(hs_r, 1)
                    if parts and parts[s]:
                        parts[s]()
                dve.wait_ge(o_out, 16 * c + 16)
                for k in range(CH):
                    dve.wait_ge(y_r, CH * c + k // 2 * 2 + 2)
                    nc.vector.scalar_tensor_tensor(out=ot[:, k, :], in0=pY[k], scalar=gtanh[:, 1:2], in1=row(xt, c, k),
                                                   op0=ALU.mult, op1=ALU.add).then_inc(o_r, 1)

            dve.wait_ge(prep_c, 3)
            schedule(dve, lambda c, par: [f or (lambda: None) for f in front(c, par)], ffn)


_INS = ['x', 'ctx_1024', 'g_xattn', 'g_ffn', 'L0_ffn_routing_W', 'L0_ffn_expert_bias', 'L0_ffn_sW1', 'L0_ffn_sb1',
        'L0_ffn_sW2', 'L0_ffn_sb2', 'L0_ffn_rW1', 'L0_ffn_rb1', 'L0_ffn_rW2', 'L0_ffn_rb2']


def kernel(**inputs):
    import numpy as _np
    import concourse.bacc as _bacc
    from concourse import mybir as _mybir
    from concourse.bass_utils import run_bass_kernel_spmd as _run

    nc = _bacc.Bacc("TRN2", target_bir_lowering=False, num_devices=1)
    arrays, args = {}, []
    for name in _INS:
        a = _np.ascontiguousarray(inputs[name])
        arrays[f"in_{name}"] = a
        args.append(nc.dram_tensor(f"in_{name}", a.shape, _mybir.dt.from_np(a.dtype), kind="ExternalInput").ap())
    o = nc.dram_tensor("out_0", inputs["x"].shape, _mybir.dt.float32, kind="ExternalOutput").ap()
    build_kernel(nc, *args, o)
    r = _run(nc, [arrays], core_ids=[0])
    return r.results[0]["out_0"]
```

```python
from contextlib import ExitStack

import concourse.bass as bass
from concourse import mybir

ALU = mybir.AluOpType
ACT = mybir.ActivationFunctionType
AX = mybir.AxisListType
F32 = mybir.dt.float32
F16 = mybir.dt.float16
BF16 = mybir.dt.bfloat16
I32 = mybir.dt.int32

P = 128
BIG = 1e30
LN_EPS = 1e-5
QB = 4
LAG = 2
RING = 4
SEG = 16
ROWS = 4
CH = 4


def build_kernel(nc, x, ctx_in, g_xattn, g_ffn, routing_W, expert_bias, sW1, sb1, sW2, sb2,
                 rW1, rb1, rW2, rb2, out):
    B, S, DM = x.shape
    E, H = rW1.shape[0], rW1.shape[2]
    NE = E + 1
    NB = 6 * E + 3
    KT = DM // P
    NCH = B // CH
    W = S // QB
    LANES = P // (QB * QB)
    T = S + LAG * (QB - 1)
    TOK = CH * S
    assert S == P and B == QB * LANES and H == P and DM == 2 * P and W == 32

    shift = [[(l - LANES * k) % 32 for l in range(32)] for k in range(QB)]

    ctx = ExitStack()
    with ctx:
        def sb(name, shape, dt=F32):
            return ctx.enter_context(nc.sbuf_tensor(name, shape, dt))

        def sem(name):
            return ctx.enter_context(nc.semaphore(name))

        xt = sb("xt", [P, B, DM])
        ct = sb("ct", [P, B, DM])
        w1 = sb("w1", [P, 2, KT, NE, H], F16)
        w2 = sb("w2", [P, 2, NE, DM], F16)
        b1row = sb("b1row", [NE, H])
        b1 = sb("b1", [P, NE])
        b2 = sb("b2", [NE, DM])
        rw = sb("rw", [E, DM])
        rwT = sb("rwT", [P, 2, KT, E], F16)
        rwF = sb("rwF", [P, KT, E])
        wsum = sb("wsum", [P, 5])
        norm = sb("norm", [P, 5])
        wscale = sb("wscale", [P, 4])
        wback = sb("wback", [P, 4])
        bound = sb("bound", [P, 2])
        hscale = sb("hscale", [P, 1])
        bscale = sb("bscale", [P, 1])
        isE = sb("isE", [P, 1])
        notE = sb("notE", [P, 1])
        pf = sb("pf", [P, 1])
        outg = sb("outg", [P, 1])
        wjunk = sb("wjunk", [P, NE])
        ebias = sb("ebias", [P, E])
        gates = sb("gates", [P, 2])
        gtanh = sb("gtanh", [P, 2])
        ident = sb("ident", [P, P])
        identb = sb("identb", [P, P], BF16)
        identh = sb("identh", [P, P], F16)
        ones = sb("ones", [P, P])
        iotaS = sb("iotaS", [P, S])
        iotaL = sb("iotaL", [P, S])
        rank = sb("rank", [P, CH, E])
        sel3 = sb("sel3", [3 * E, E, P], BF16)
        arenaT = sb("arenaT", [P, S * S // 2])
        arenaD = sb("arenaD", [P, (W + 1) * T])
        arenaA = sb("arenaA", [P, T * W])
        arenaI = sb("arenaI", [P, T * W])
        arenaF = sb("arenaF", [P, (T + 1) * W + T * W // 2])
        XT = 2 * CH * DM
        xnT = arenaT[:, 0:XT].rearrange("p (r k d) -> p r k d", r=2, k=CH)
        cT = arenaT[:, XT:2 * XT].rearrange("p (r k d) -> p r k d", r=2, k=CH)
        xn = arenaT[:, 2 * XT:3 * XT].rearrange("p (r k d) -> p r k d", r=2, k=CH)
        d2 = arenaT[:, 3 * XT:3 * XT + CH * S].rearrange("p (k s) -> p k s", k=CH)
        sq = arenaF[:, 0:XT].rearrange("p (r k d) -> p r k d", r=2, k=CH)
        w1f = arenaT[:, 0:KT * NE * H].rearrange("p (k e h) -> p k e h", k=KT, e=NE)
        w1s = arenaT[:, KT * NE * H:2 * KT * NE * H]
        turnedLF = arenaT[:, 2 * KT * NE * H:2 * KT * NE * H + 2 * SEG * W].rearrange("p (r w) -> p r w", r=2)
        BO = 2 * KT * NE * H + 2 * SEG * W
        b2rest = arenaT[0:NE, BO:BO + DM]
        b2part = arenaT[0:NE, BO + DM:BO + DM + 3 * DM // 2].bitcast(BF16).rearrange("p (a d) -> p a d", a=3)
        table = arenaT[:, :].bitcast(F16).rearrange("p (i w) -> p i w", w=S)
        Dall = arenaD[:, :].rearrange("p (w t) -> p w t", t=T)
        V2 = arenaD[:, :].rearrange("p (t w) -> p t w", w=W + 1)
        Dst = arenaA[:, 0:B * S].rearrange("p (b s) -> p b s", b=B)
        cand = arenaA[:, :]
        candv = cand.rearrange("p (t w) -> p t w", w=W)
        iotaJ = arenaI[:, :]
        lowm = arenaI[:, 0:B * S].rearrange("p (b s) -> p b s", b=B)
        FW = (T + 1) * W // 2
        DL = arenaF[:, 0:FW].bitcast(F16)
        LF = arenaF[:, FW:2 * FW].bitcast(F16)
        dV = arenaF[:, 2 * FW:2 * FW + T * W // 2].bitcast(F16)
        sqs = arenaF[:, XT:XT + 2 * CH * S].rearrange("p (r k s) -> p r k s", r=2, k=CH)
        x2T = arenaA[:, 0:2 * KT * TOK].bitcast(F16).rearrange("p (r k n) -> p r k n", r=2, k=2 * KT)
        xn2h = arenaA[:, 2 * KT * TOK:2 * KT * TOK + CH * DM // 2].bitcast(F16).rearrange("p (k d) -> p k d", k=CH)
        xn2l = arenaA[:, 2 * KT * TOK + CH * DM // 2:2 * KT * TOK + CH * DM].bitcast(F16).rearrange("p (k d) -> p k d", k=CH)
        xn2 = arenaD[:, 0:CH * DM].rearrange("p (k d) -> p k d", k=CH)
        hid = arenaD[:, CH * DM:CH * DM + 2 * TOK].rearrange("p (r n) -> p r n", r=2)
        hsc = arenaD[:, CH * DM + 2 * TOK:CH * DM + 4 * TOK].rearrange("p (r n) -> p r n", r=2)
        ot = arenaF[:, 0:CH * DM].rearrange("p (k d) -> p k d", k=CH)
        HO = CH * DM + TOK
        halves = arenaF[:, HO:HO + 3 * TOK].bitcast(F16).rearrange("p (r a n) -> p r a n", r=3, a=2)
        w2f = arenaA[:, T * W - NE * DM:]
        w2fv = w2f.rearrange("p (e d) -> p e d", e=NE)
        mask = arenaD[:, CH * DM + 5 * TOK:CH * DM + 6 * TOK].rearrange("p (k s) -> p k s", k=CH)
        cfT = arenaF[0:NB, CH * DM:CH * DM + TOK].bitcast(BF16).rearrange("p (r n) -> p r n", r=2)
        dVv = dV.rearrange("p (t w) -> p t w", w=W)
        st = sb("st", [P, CH, 6])
        mv = sb("mv", [P, 2, CH, 2])
        bb = sb("bb", [P, B])
        R = sb("R", [P, RING, W + 1])
        M = sb("M", [P, RING, W + 1])
        pidx = sb("pidx", [P, 1], I32)
        qidx = sb("qidx", [P, 1], I32)
        qf = sb("qf", [P, 1])
        edgeD = sb("edgeD", [P, 1])
        edgeR = sb("edgeR", [P, 1])
        base = sb("base", [P, 1])
        left = sb("left", [P, QB - 1, T])
        spreadM = sb("spreadM", [P, QB, P], F16)
        VH = sb("VH", [P, S + 1])
        hiC = sb("hiC", [P, B])
        loC = sb("loC", [P, B])
        junk = sb("junk", [P, S])
        var2 = sb("var2", [P, 2, CH])
        neghalf = sb("neghalf", [P, CH])
        half = sb("half", [P, CH * E])
        rstd2 = sb("rstd2", [P, 2, CH])
        lg = sb("lg", [P, CH, E])
        mag = sb("mag", [P, CH, E])
        ex = sb("ex", [P, CH, E])
        ln = sb("ln", [P, CH, E])
        sp = sb("sp", [P, CH, E])
        root = sb("root", [P, 2, CH])
        m1 = sb("m1", [P, 2, CH])
        eq = sb("eq", [P, CH, E])
        i1 = sb("i1", [P, CH])
        oh = sb("oh", [P, CH, E])
        oh2 = sb("oh2", [P, CH, E])
        a2 = sb("a2", [P, CH, E])
        gate = sb("gate", [P, CH, E])
        usum = sb("usum", [P, CH, E])
        uerr = sb("uerr", [P, CH, E])
        res = sb("res", [P, CH, E])
        cf = sb("cf", [P, CH, NB], BF16)
        cfb = cf[:, :, 0:6 * E].rearrange("p k (b e) -> p k b e", e=E)
        bias = sb("bias", [NB, DM], BF16)

        bank = [ctx.enter_context(nc.psum_tensor(f"bank{i}", [P, 512], F32)) for i in range(8)]

        consts = sem("consts")
        x_in = [sem(f"x_in{i}") for i in range(2)]
        c_in = [sem(f"c_in{i}") for i in range(NCH)]
        w_in, passed = sem("w_in"), sem("passed")
        spilled = [sem(f"spilled{i}") for i in range(NCH)]
        lane_c = sem("lane_c")
        prep_T, prep_c = sem("prep_T"), sem("prep_c")
        dstep = sem("dstep")
        stats, bbs, xn_r, xnT_ps, xnT_r = (sem(n) for n in ("stats", "bbs", "xn_r", "xnT_ps", "xnT_r"))
        cT_ps, cT_r, sq_r, ab_r, d2_r, dst_r, dall = (sem(n) for n in (
            "cT_ps", "cT_r", "sq_r", "ab_r", "d2_r", "dst_r", "dall"))
        dall_init = sem("dall_init")
        chain = sem("chain")
        chosen = sem("chosen")
        norms, hi2_r, hl_r, own_r = sem("norms"), sem("hi2_r"), sem("hl_r"), sem("own_r")
        w_split, wsum_r, wscale_r, rwF_r = sem("w_split"), sem("wsum_r"), sem("wscale_r"), sem("rwF_r")
        hi_r, lo_r, sqh_r = sem("hi_r"), sem("lo_r"), sem("sqh_r")
        flag, mins, costs = sem("flag"), sem("mins"), sem("costs")
        bulk, turned, cand_r, dV_r, tab_ps, tab_r, spread_r = (sem(n) for n in (
            "bulk", "turned", "cand_r", "dV_r", "tab_ps", "tab_r", "spread_r"))
        b_part, b_in = sem("b_part"), sem("b_in")
        zero_r, above_r, relu_r, part_r = (sem(n) for n in ("zero_r", "above_r", "relu_r", "part_r"))
        walk = sem("walk")
        vT, vTc, low_r = sem("vT"), sem("vTc"), sem("low_r")
        mask_r, al, x1_r, st2, mv2, ve, rs2, xn2_r, x2_ps, x2_r = (sem(n) for n in (
            "mask_r", "al", "x1_r", "st2", "mv2", "ve", "rs2", "xn2_r", "x2_ps", "x2_r"))
        lg_ps, lg_r, spa, spb, pw, rt, cfT_ps, cfT_r = (sem(n) for n in (
            "lg_ps", "lg_r", "spa", "spb", "pw", "rt", "cfT_ps", "cfT_r"))
        h_ps, h_r, cb_ps, hs_r, y_e, y_r, o_r, o_out = (sem(n) for n in (
            "h_ps", "h_r", "cb_ps", "hs_r", "y_e", "y_r", "o_r", "o_out"))

        dist = nc.dram_tensor("dist", (B, S, S), F32, kind="Internal").ap()

        block = ctx.enter_context(nc.Block())

        x_v = x.rearrange("b s d -> s b d")
        c_v = ctx_in.rearrange("b s d -> s b d")
        o_v = out.rearrange("b s d -> s b d")
        N_W = 12

        pXT = [bank[k][:, 0:DM] for k in range(2)]
        pCT = [bank[2 + k][:, 0:DM] for k in range(2)]
        pAB = [bank[CH + k][:, 0:S] for k in range(CH)]
        pPrep = bank[3]
        pSum = bank[2][:, 0:4]
        pTab = [bank[4 + k][:, :].rearrange("p (q w) -> p q w", q=QB) for k in range(4)]
        BEFORE = 9
        NTAB = S // ROWS
        NSEG = S // SEG
        TAIL = NSEG * SEG
        CUT = 3 * S // 4
        PARTS = [(CUT - 32 * (n + 1), CUT - 32 * n) for n in range(3)]
        pE = [bank[k // 2][:, DM * (k % 2):DM * (k % 2) + DM] for k in range(CH)]
        pLg = bank[0][:, DM:DM + CH * E].rearrange("p (k e) -> p k e", e=E)
        pX = [bank[k][:, 0:DM].bitcast(F16) for k in range(2)]
        pC = bank[1][0:NB, 0:TOK // 2].bitcast(BF16)
        pH = [bank[2][:, :], bank[3][:, :]]
        pCb = [bank[4][:, :], bank[7][:, :]]
        pY = [bank[5 + k // 2][:, DM * (k % 2):DM * (k % 2) + DM] for k in range(CH)]

        def col(tile, c, k):
            return tile[:, bass.ds(CH * c + k, 1)] if not isinstance(c, int) else tile[:, CH * c + k:CH * c + k + 1]

        def row(tile, c, k):
            if isinstance(c, int):
                return tile[:, CH * c + k, :]
            return tile[:, bass.ds(CH * c + k, 1), :].rearrange("p a n -> p (a n)")

        def hbuf(par, s):
            return (par + s) % 2

        def schedule(eng, front, ffn):
            for part in front(0, 0):
                part()
            ffn(0, 0, front(1, 1))
            with eng.Fori(0, NCH // 2 - 2) as n:
                ffn(2 * n + 1, 1, front(2 * n + 2, 0))
                ffn(2 * n + 2, 0, front(2 * n + 3, 1))
            ffn(NCH - 3, 1, front(NCH - 2, 0))
            ffn(NCH - 2, 0, front(NCH - 1, 1))
            ffn(NCH - 1, 1, [])

        def first_chunk(c):
            return isinstance(c, int) and c == 0

        def pipeline(eng, first, second):
            first(0, 0)
            with eng.Fori(0, NCH // 2 - 1) as n:
                for r in range(2):
                    first(2 * n + r + 1, 1 - r)
                    second(2 * n + r, r)
            first(NCH - 1, 1)
            second(NCH - 2, 0)
            second(NCH - 1, 1)

        def fetch(eng, g, blocks):
            for c in range(g * LANES // CH, (g + 1) * LANES // CH):
                eng.wait_ge(spilled[c], 16)
            for q in blocks:
                lane = 32 * g + LANES * q
                eng.dma_start(Dall[lane:lane + LANES, 1:W + 1, LAG * q:LAG * q + S],
                              dist[LANES * g:LANES * g + LANES, W * q:W * q + W, :]).then_inc(dall, 16)

        @block.sync
        def _(sync):
            def load(c):
                if c >= 2:
                    sync.wait_ge(x_in[c % 2], 16 * (c // 2))
                sync.dma_start(xt[:, CH * c:CH * c + CH, :], x_v[:, CH * c:CH * c + CH, :]).then_inc(x_in[c % 2], 16)

            def spill(c):
                sync.wait_ge(dst_r, CH * c + 2 * CH)
                sync.dma_start(dist[CH * c:CH * c + CH].rearrange("b w s -> w b s"),
                               Dst[:, CH * c:CH * c + CH, :]).then_inc(spilled[c], 16)

            for c in range(4):
                load(c)
            sync.wait_ge(dall_init, 2)
            for c in range(NCH):
                if c + 4 < NCH:
                    load(c + 4)
                spill(c)
                if c % 2:
                    fetch(sync, c // 2, range(QB) if c < NCH - 1 else range(0, QB, 2))
            sync.wait_ge(b_part, 5)
            for r, part in enumerate((0, 0, 0, 1, 2, 1)):
                sync.dma_start(bias[E * r:E * r + E, :], b2part[0:E, part, :]).then_inc(b_in, 16)
            for part in range(3):
                sync.dma_start(bias[6 * E + part:6 * E + part + 1, :], b2part[E:NE, part, :]).then_inc(b_in, 16)
            with sync.Fori(0, NCH) as c:
                sync.wait_ge(o_r, CH * c + 2 * CH)
                sync.dma_start(o_v[:, bass.ds(CH * c, CH), :], ot[:, :, :]).then_inc(o_out, 16)
            sync.wait_ge(o_out, 16 * NCH + 16)

        @block.gpsimd
        def _(pool):
            nc.gpsimd.memset(ident[:, :], 0.0).then_inc(lane_c, 1)
            nc.gpsimd.iota(pidx[:, :], pattern=[[0, 1]], base=0, channel_multiplier=1).then_inc(consts, 1)
            nc.gpsimd.memset(ones[:, :], 1.0).then_inc(consts, 1)
            pool.wait_ge(lane_c, 1)
            nc.gpsimd.affine_select(out=ident[:, :], in_=ident[:, :], compare_op=ALU.not_equal, fill=1.0,
                                    base=0, pattern=[[-1, P]], channel_multiplier=1).then_inc(consts, 1)
            nc.gpsimd.memset(neghalf[:, :], -0.5).then_inc(consts, 1)
            nc.gpsimd.iota(iotaJ.rearrange("p (t w) -> p t w", w=W), pattern=[[2 * S, T], [1, W]], base=0,
                           channel_multiplier=0, allow_small_or_imprecise_dtypes=True).then_inc(consts, 1)
            def root_of(c):
                pool.wait_ge(stats, 2 * CH * c + 2 * CH)
                nc.gpsimd.tensor_scalar(var2[:, c % 2, :], mv[:, c % 2, :, 1], LN_EPS, None, ALU.add).then_inc(ve, 1)
                pool.wait_ge(ve, c + 1)
                nc.gpsimd.tensor_tensor(rstd2[:, c % 2, :], var2[:, c % 2, :], neghalf[:, :], ALU.pow).then_inc(rs2, 1)

            def squares(c):
                r = c % 2
                for k in range(CH):
                    pool.wait_ge(sqh_r, CH * c + k + 1)
                    nc.gpsimd.tensor_tensor(sqs[:, r, k, :], sq[:, r, k, 0:P], sq[:, r, k, P:DM], ALU.add).then_inc(sq_r, 1)

            root_of(0)
            root_of(1)
            for c in range(NCH):
                squares(c)
                if c + 2 < NCH:
                    root_of(c + 2)
            nc.gpsimd.memset(sel3[:, :, :], 0.0).then_inc(lane_c, 1)
            nc.gpsimd.memset(half[:, :], 0.5).then_inc(consts, 1)
            nc.gpsimd.iota(iotaS[:, :], pattern=[[1, S]], base=0, channel_multiplier=0,
                           allow_small_or_imprecise_dtypes=True).then_inc(consts, 1)
            nc.gpsimd.iota(rank[:, :, :], pattern=[[0, CH], [-1, E]], base=E, channel_multiplier=0,
                           allow_small_or_imprecise_dtypes=True).then_inc(consts, 1)
            nc.gpsimd.iota(iotaL[:, :], pattern=[[1, S]], base=0, channel_multiplier=0,
                           allow_small_or_imprecise_dtypes=True).then_inc(lane_c, 1)
            pool.wait_ge(lane_c, 3)
            nc.gpsimd.memset(iotaL[:, 0:1], BIG).then_inc(consts, 1)
            for k in range(3):
                pool.wait_ge(lane_c, 3 + k)
                nc.gpsimd.affine_select(out=sel3[:, :, :], in_=sel3[:, :, :], compare_op=ALU.not_equal, fill=1.0,
                                        base=-E * k, pattern=[[-1, E], [0, P]],
                                        channel_multiplier=1).then_inc(lane_c if k < 2 else consts, 1)
            pool.wait_ge(dall, 16 * QB * QB)
            pool.dma_start(w1f[:, :, E, :], sW1.rearrange("(k p) h -> p k h", p=P)).then_inc(w_in, 16)
            for k in range(KT):
                pool.dma_start(w1f[:, k, 0:E, :],
                               rW1[:, P * k:P * k + P, :].rearrange("e p h -> p e h")).then_inc(w_in, 16)
            pool.dma_start(w2fv[:, E, :], sW2).then_inc(w_in, 16)
            pool.dma_start(w2fv[:, 0:E, :], rW2.rearrange("e h d -> h e d")).then_inc(w_in, 16)
            pool.dma_start(b1row[0:E, :], rb1).then_inc(w_in, 16)
            pool.dma_start(b1row[E:NE, :], sb1.rearrange("(a h) -> a h", a=1)).then_inc(w_in, 16)
            pool.dma_start(b2[0:E, :], rb2).then_inc(w_in, 16)
            pool.dma_start(b2[E:NE, :], sb2.rearrange("(a h) -> a h", a=1)).then_inc(w_in, 16)
            pool.dma_start(rw[:, :], routing_W).then_inc(w_in, 16)
            pool.dma_start(ebias[:, :],
                           expert_bias.rearrange("(a e) -> a e", a=1).to_broadcast([P, E])).then_inc(w_in, 16)
            pool.dma_start(gates[:, 0:1], g_xattn.rearrange("(a e) -> a e", a=1).to_broadcast([P, 1])).then_inc(w_in, 16)
            pool.dma_start(gates[:, 1:2], g_ffn.rearrange("(a e) -> a e", a=1).to_broadcast([P, 1])).then_inc(w_in, 16)
            count = [0]

            def own(ins):
                ins.then_inc(own_r, 1)
                count[0] += 1
                pool.wait_ge(own_r, count[0])

            pool.wait_ge(wsum_r, 6)
            own(nc.gpsimd.tensor_scalar(wsum[:, :], wsum[:, :], 1e-20, None, ALU.max))
            own(nc.gpsimd.tensor_tensor(wscale[:, 0:3], wsum[:, 0:3], neghalf[:, 0:3], ALU.pow))
            nc.gpsimd.tensor_scalar(wscale[:, 0:3], wscale[:, 0:3], 16384.0, None, ALU.mult).then_inc(wscale_r, 1)
            own(nc.gpsimd.tensor_tensor(norm[:, :], wsum[:, :], half[:, 0:5], ALU.pow))
            own(nc.gpsimd.tensor_scalar(bound[:, :], norm[:, 0:2], float(DM) ** 0.5, None, ALU.mult))
            own(nc.gpsimd.tensor_tensor(bound[:, :], bound[:, :], norm[:, 3:5], ALU.add))
            own(nc.gpsimd.tensor_scalar(bound[:, 1:2], bound[:, 1:2], 1.0, None, ALU.add))
            own(nc.gpsimd.tensor_tensor(hscale[:, :], bound[:, 0:1], bound[:, 0:1], ALU.mult))
            own(nc.gpsimd.tensor_tensor(hscale[:, :], hscale[:, :], bound[:, 1:2], ALU.mult))
            own(nc.gpsimd.tensor_tensor(hscale[:, :], hscale[:, :], neghalf[:, 0:1], ALU.pow))
            own(nc.gpsimd.tensor_scalar(hscale[:, :], hscale[:, :], 16384.0, None, ALU.mult))
            pool.wait_ge(wscale_r, 1)
            nc.gpsimd.tensor_tensor(wscale[:, 3:4], wscale[:, 2:3], hscale[:, :], ALU.mult).then_inc(wscale_r, 1)
            own(nc.gpsimd.tensor_tensor(bscale[:, :], isE[:, :], hscale[:, :], ALU.mult))
            own(nc.gpsimd.tensor_tensor(bscale[:, :], bscale[:, :], notE[:, :], ALU.add))
            nc.gpsimd.tensor_tensor(bscale[:, :], bscale[:, :], wscale[:, 2:3], ALU.mult).then_inc(wscale_r, 1)
            pool.wait_ge(w_split, 6)
            nc.gpsimd.tensor_tensor(w1[:, 1, :, :, :].rearrange("p k e h -> p (k e h)"), w1s,
                                    w1[:, 0, :, :, :].rearrange("p k e h -> p (k e h)"), ALU.subtract).then_inc(w_split, 1)
            nc.gpsimd.tensor_tensor(rwT[:, 1, :, :], rwF[:, :, :], rwT[:, 0, :, :], ALU.subtract).then_inc(w_split, 1)
            nc.gpsimd.tensor_tensor(w2[:, 1, :, :].rearrange("p e d -> p (e d)"), w2f,
                                    w2[:, 0, :, :].rearrange("p e d -> p (e d)"), ALU.subtract).then_inc(w_split, 1)
            for part in range(2):
                pool.wait_ge(b_part, 2 * part + 1)
                nc.gpsimd.tensor_tensor(b2rest, b2rest if part else b2[:, :], b2part[:, part, :],
                                        ALU.subtract).then_inc(b_part, 1)
            for n in range(NSEG):
                here = slice(W * SEG * n, W * SEG * (n + 1))
                pool.wait_ge(turned, 2 * n + 1)
                nc.gpsimd.tensor_tensor(cand[:, here], cand[:, here], iotaJ[:, here], ALU.add).then_inc(cand_r, 1)
                pool.wait_ge(turned, 2 * n + 2)
                pool.wait_ge(cand_r, 2 * n + 1)
                nc.gpsimd.tensor_tensor(cand[:, here], cand[:, here], turnedLF[:, n % 2, :], ALU.add).then_inc(cand_r, 1)
            pool.wait_ge(costs, T + 1)
            nc.gpsimd.memset(V2[:, 0:CUT, 0:1], 0.0).then_inc(zero_r, 1)
            pool.wait_ge(bulk, BEFORE)

            def above(n):
                lo, hi = PARTS[n]
                nc.gpsimd.tensor_tensor(candv[:, lo:hi, :], candv[:, lo:hi, :],
                                        left[:, 0, lo:hi].unsqueeze(2).to_broadcast([P, hi - lo, W]),
                                        ALU.subtract).then_inc(above_r, 1)

            def increments(n):
                lo, hi = PARTS[n]
                pool.wait_ge(zero_r, 1)
                pool.wait_ge(relu_r, n + 1)
                nc.gpsimd.tensor_tensor(dVv[:, lo:hi, :], V2[:, lo:hi, 1:W + 1], V2[:, lo:hi, 0:W],
                                        ALU.subtract).then_inc(part_r, 1)

            above(0)
            above(1)
            increments(0)
            above(2)
            increments(1)
            increments(2)
            pool.wait_ge(vTc, 2)
            for c in range(NCH):
                for k in range(CH):
                    nc.gpsimd.tensor_scalar(row(lowm, c, k), iotaS[:, :], col(loC, c, k), None,
                                            ALU.is_lt).then_inc(low_r, 1)
                pool.wait_ge(mv2, CH * c + CH)
                nc.gpsimd.tensor_scalar(var2[:, 0, :], mv[:, 0, :, 1], LN_EPS, None, ALU.add).then_inc(ve, 1)
                pool.wait_ge(ve, NCH + c + 1)
                nc.gpsimd.tensor_tensor(rstd2[:, 0, :], var2[:, 0, :], neghalf[:, :], ALU.pow).then_inc(rs2, 1)
                for k in range(CH):
                    pool.wait_ge(hi_r, CH * c + k + 1)
                    nc.gpsimd.tensor_tensor(xn2l[:, k, :], xn2[:, k, :], xn2h[:, k, :], ALU.subtract).then_inc(lo_r, 1)
                pool.wait_ge(chosen, c + 1)
                nc.gpsimd.tensor_tensor(root[:, :, :], m1[:, :, :], half[:, 0:2 * CH].rearrange("p (a k) -> p a k", a=2),
                                        ALU.pow).then_inc(pw, 1)

        @block.scalar
        def _(act):
            for c in range(NCH):
                act.dma_start(ct[:, CH * c:CH * c + CH, :], c_v[:, CH * c:CH * c + CH, :]).then_inc(c_in[c], 16)
            nc.scalar.preload_act_table_set("sqrt_and_others")

            def evacuate(c, par):
                for k in range(CH):
                    act.wait_ge(xnT_ps, CH * c + k + 1)
                    nc.scalar.mul(xnT[:, par, k, :], pXT[k % 2], -2.0).then_inc(xnT_r, 1)
                    act.wait_ge(cT_ps, CH * c + k + 1)
                    nc.scalar.activation(sq[:, par, k, :], pCT[k % 2], ACT.Square).then_inc(sqh_r, 1)
                    nc.scalar.copy(cT[:, par, k, :], pCT[k % 2]).then_inc(cT_r, 1)

            def roots(c, par):
                for k in range(CH):
                    act.wait_ge(d2_r, CH * c + k + 1 + CH)
                    nc.scalar.activation(row(Dst, c, k), d2[:, k, :], ACT.Sqrt).then_inc(dst_r, 1)

            pipeline(act, evacuate, roots)
            fetch(act, QB - 1, range(1, QB, 2))
            nc.scalar.preload_act_table_set("silu_and_others")
            act.wait_ge(w_in, 16 * 13)
            nc.scalar.activation(w1s, arenaT[:, 0:KT * NE * H], ACT.Square, accum_out=wsum[:, 0:1]).then_inc(wsum_r, 1)
            act.wait_ge(prep_T, 1)
            nc.scalar.copy(rwF[:, :, :], pPrep[:, 0:KT * E].rearrange("p (k e) -> p k e", e=E)).then_inc(rwF_r, 1)
            nc.scalar.copy(b1[:, :], pPrep[:, 32:32 + NE]).then_inc(rwF_r, 1)
            act.wait_ge(rwF_r, 2)
            nc.scalar.activation(wjunk[:, :], b1[:, :], ACT.Square, accum_out=wsum[:, 3:4]).then_inc(wsum_r, 1)
            act.wait_ge(wsum_r, 2)
            nc.scalar.activation(wjunk[:, 0:E], ebias[:, :], ACT.Square, accum_out=wsum[:, 4:5]).then_inc(wsum_r, 1)
            nc.scalar.activation(w1s, w2f, ACT.Square, accum_out=wsum[:, 2:3]).then_inc(wsum_r, 1)
            act.wait_ge(wsum_r, 4)
            nc.scalar.activation(w1s[:, 0:KT * E], rwF[:, :, :].rearrange("p k e -> p (k e)"), ACT.Square,
                                 accum_out=wsum[:, 1:2]).then_inc(wsum_r, 1)
            act.wait_ge(prep_T, 2)
            nc.scalar.copy(wsum[:, 0:4], pSum).then_inc(wsum_r, 1)
            act.wait_ge(wscale_r, 1)
            nc.scalar.mul(w1s, arenaT[:, 0:KT * NE * H], wscale[:, 0:1]).then_inc(w_split, 1)
            nc.scalar.mul(rwF[:, :, :], rwF[:, :, :], wscale[:, 1:2]).then_inc(w_split, 1)
            nc.scalar.mul(w2f, w2f, wscale[:, 2:3]).then_inc(w_split, 1)
            act.wait_ge(w_split, 3)
            nc.scalar.copy(w1[:, 0, :, :, :].rearrange("p k e h -> p (k e h)"), w1s).then_inc(w_split, 1)
            nc.scalar.copy(rwT[:, 0, :, :], rwF[:, :, :]).then_inc(w_split, 1)
            nc.scalar.copy(w2[:, 0, :, :].rearrange("p e d -> p (e d)"), w2f).then_inc(w_split, 1)
            act.wait_ge(wscale_r, 3)
            nc.scalar.mul(b2[:, :], b2[:, :], bscale[0:NE, 0:1]).then_inc(norms, 1)
            nc.scalar.activation(gtanh[:, :], gates[:, :], ACT.Tanh).then_inc(prep_c, 1)

            def front(c, par):
                def turn():
                    for k in range(CH):
                        act.wait_ge(x2_ps, CH * c + k + 1)
                        nc.scalar.copy(x2T[:, par, :, S * k:S * k + S],
                                       pX[k % 2].rearrange("p (k n) -> p k n", n=S)).then_inc(x2_r, 1)

                def softplus():
                    nc.scalar.preload_act_table_set("natural_log_exp_and_others")
                    act.wait_ge(lg_r, 2 * c + 2)
                    nc.scalar.activation(ex[:, :, :], mag[:, :, :], ACT.Exp, scale=-1.0).then_inc(spa, 1)
                    act.wait_ge(spa, 2 * c + 1)
                    nc.scalar.activation(ln[:, :, :], ex[:, :, :], ACT.Ln, bias=1.0).then_inc(spa, 1)
                    nc.scalar.preload_act_table_set("silu_and_others")


                def high_halves():
                    for k in range(CH):
                        act.wait_ge(xn2_r, CH * c + k + 1)
                        nc.scalar.copy(xn2h[:, k, :], xn2[:, k, :]).then_inc(hi_r, 1)
                return [None, None, None, high_halves, turn, softplus, None, None, None]

            def high(c, par, s):
                if s >= 3:
                    act.wait_ge(y_e, E * c + s - 2)
                elif not first_chunk(c):
                    if s == 2:
                        act.wait_ge(y_r, CH * c)
                    else:
                        act.wait_ge(y_e, E * c + s - 1)
                if s == 0:
                    act.wait_ge(h_r, NE * c + 3)
                    nc.scalar.mul(halves[:, 0, 0, :], hid[:, par, :], hscale[:, 0:1]).then_inc(hi2_r, 1)
                else:
                    act.wait_ge(hs_r, E * c + s + 1)
                    nc.scalar.copy(halves[:, s % 3, 0, :], hsc[:, (s - 1) % 2, :]).then_inc(hi2_r, 1)

            def ffn(c, par, parts):
                for s in range(NE):
                    if s >= 1:
                        high(c, par, s - 1)
                    elif not first_chunk(c):
                        high(c - 1, 1 - par, NE - 1)
                    act.wait_ge(h_ps, NE * c + s + 1)
                    if s == 2:
                        act.wait_ge(hl_r, NE * c + 1)
                    elif s > 2:
                        act.wait_ge(hs_r, E * c + s - 1)
                    elif not first_chunk(c):
                        act.wait_ge(hs_r, E * c + s)
                    nc.scalar.activation(hid[:, hbuf(par, s), :], pH[hbuf(par, s)], ACT.Silu,
                                         bias=b1[:, (s - 1) % NE:(s - 1) % NE + 1], scale=wback[:, 0:1]).then_inc(h_r, 1)
                    if s == 0:
                        act.wait_ge(cfT_ps, c + 1)
                        nc.scalar.copy(cfT[:, par, :], pC).then_inc(cfT_r, 1)
                    if parts:
                        parts[s]()

            act.wait_ge(norms, 1)
            for part in range(3):
                if part:
                    act.wait_ge(b_part, 2 * part)
                nc.scalar.copy(b2part[:, part, :], b2rest if part else b2[:, :]).then_inc(b_part, 1)
            for q in range(QB):
                nc.scalar.copy(spreadM[:, q, :].rearrange("p (g a b) -> p g a b", g=QB, a=QB),
                               ident[:, :].rearrange("p (g a b) -> p g a b", g=QB, a=QB)[:, :, q:q + 1, :]
                               .to_broadcast([P, QB, QB, LANES])).then_inc(spread_r, 1)
            for n in range(NSEG):
                here = slice(W * SEG * n, W * SEG * (n + 1))
                act.wait_ge(flag, SEG * (n + 1) + 1)
                nc.scalar.mul(cand[:, here], DL[:, here], -0.75).then_inc(turned, 1)
                if n >= 2:
                    act.wait_ge(cand_r, 2 * n - 2)
                nc.scalar.mul(turnedLF[:, n % 2, :], LF[:, W * (SEG * n + 1):W * (SEG * (n + 1) + 1)],
                              -1000.0).then_inc(turned, 1)
            act.wait_ge(w_split, 7)
            act.wait_ge(b_in, 16 * 9)
            act.wait_ge(cand_r, 2 * NSEG)
            for n in range(NTAB):
                i = S - ROWS * (n + 1)
                if n in (4, 8, 12):
                    lo, hi = PARTS[n // 4 - 1]
                    act.wait_ge(above_r, n // 4)
                    nc.scalar.activation(V2[:, lo:hi, 1:W + 1], candv[:, lo:hi, :], ACT.Relu).then_inc(relu_r, 1)
                act.wait_ge(tab_ps, n + 1)
                nc.scalar.copy(table[:, i:i + ROWS, :].rearrange("p i (q w) -> p q i w", q=QB),
                               pTab[n % 4].rearrange("p q (i w) -> p q i w", i=ROWS)).then_inc(tab_r, 1)
            act.wait_ge(vTc, 2)
            act.wait_ge(prep_c, 2)
            schedule(act, lambda c, par: [f or (lambda: None) for f in front(c, par)], ffn)
            high(NCH - 1, 1, NE - 1)

        @block.tensor
        def _(pe):
            pe.wait_ge(consts, 3)
            def turn_chunk(c):
                pe.wait_ge(c_in[c], 16)
                for k in range(CH):
                    pe.wait_ge(xn_r, CH * c + k + 1)
                    pe.wait_ge(xnT_r, CH * c + k + 1)
                    nc.tensor.transpose(pXT[k % 2][:, 0:P], xn[:, c % 2, k, 0:P], ident[:, :])
                    nc.tensor.transpose(pXT[k % 2][:, P:DM], xn[:, c % 2, k, P:DM], ident[:, :]).then_inc(xnT_ps, 1)
                    pe.wait_ge(cT_r, CH * c + k + 1)
                    nc.tensor.transpose(pCT[k % 2][:, 0:P], row(ct, c, k)[:, 0:P], ident[:, :])
                    nc.tensor.transpose(pCT[k % 2][:, P:DM], row(ct, c, k)[:, P:DM], ident[:, :]).then_inc(cT_ps, 1)

            def square_distances(c):
                for k in range(CH):
                    pe.wait_ge(xnT_r, CH * c + k + 1 + 2)
                    pe.wait_ge(cT_r, CH * c + k + 1 + 2)
                    pe.wait_ge(d2_r, CH * c + k + 1)
                    for i in range(KT):
                        nc.tensor.matmul(pAB[k], xnT[:, c % 2, k, P * i:P * i + P], cT[:, c % 2, k, P * i:P * i + P],
                                         start=(i == 0), stop=False)
                    pe.wait_ge(sq_r, CH * c + k + 1)
                    mm = nc.tensor.matmul(pAB[k], ones[:, :], sqs[:, c % 2, k, :], start=False, stop=True)
                    mm.then_inc(ab_r, 1)

            turn_chunk(0)
            for c in range(NCH):
                if c + 1 < NCH:
                    turn_chunk(c + 1)
                square_distances(c)
            pe.wait_ge(w_in, 16 * 13)
            for k in range(KT):
                nc.tensor.transpose(pPrep[:, E * k:E * k + E], rw[:, P * k:P * k + P], ident[0:E, 0:E])
            nc.tensor.transpose(pPrep[:, 32:32 + NE], b1row[:, :], ident[0:NE, 0:NE]).then_inc(prep_T, 1)
            pe.wait_ge(wsum_r, 5)
            nc.tensor.matmul(pSum, ones[:, :], wsum[:, 0:4], start=True, stop=True).then_inc(prep_T, 1)
            pe.wait_ge(spread_r, QB)
            for n in range(NTAB):
                i = S - ROWS * (n + 1)
                pe.wait_ge(dV_r, 2)
                if i < CUT:
                    pe.wait_ge(part_r, sum(i < hi for lo, hi in PARTS))
                if n >= 4:
                    pe.wait_ge(tab_r, n - 3)
                for q in range(QB):
                    first = W * (i + LAG * q)
                    mm = nc.tensor.matmul(pTab[n % 4][:, q, :], spreadM[:, q, :], dV[:, first:first + ROWS * W],
                                          start=True, stop=True)
                mm.then_inc(tab_ps, 1)
            pe.wait_ge(walk, S + 1)
            nc.tensor.transpose(pPrep[:, 0:P], VH[:, 1:S + 1], ident[:, :])
            nc.tensor.transpose(pPrep[:, P:2 * P], VH[:, 0:S], ident[:, :]).then_inc(vT, 1)

            def products(o, lhsT, rhs):
                for i in range(KT):
                    nc.tensor.matmul(o, lhsT(0, i), rhs(0, i), start=(i == 0), stop=False)
                    nc.tensor.matmul(o, lhsT(0, i), rhs(1, i), start=False, stop=False)
                    mm = nc.tensor.matmul(o, lhsT(1, i), rhs(0, i), start=False, stop=(i == KT - 1))
                return mm

            def front(c, par):
                def align(k):
                    pe.wait_ge(mask_r, CH * c + k + 1)
                    if k == CH // 2:
                        pe.wait_ge(cfT_r, c + 1)
                    nc.tensor.matmul(pE[k], mask[:, k, :], row(ct, c, k), start=True, stop=True).then_inc(al, 1)

                def turn():
                    for k in range(CH):
                        pe.wait_ge(lo_r, CH * c + k + 1)
                        pe.wait_ge(x2_r, CH * c + k + 1)
                        for i, part in enumerate((xn2h, xn2l)):
                            for n in range(KT):
                                o = S * (KT * i + n)
                                mm = nc.tensor.transpose(pX[k % 2][:, o:o + S], part[:, k, P * n:P * n + P], identh[:, :])
                        mm.then_inc(x2_ps, 1)

                def logits():
                    pe.wait_ge(x2_r, CH * c + CH + 2)
                    for k in range(CH):
                        mm = products(pLg[:, k, :], lambda half, i: x2T[:, par, KT * half + i, S * k:S * k + S],
                                 lambda half, i: rwT[:, half, i, :])
                    mm.then_inc(lg_ps, 1)

                return [lambda: (align(0), align(1)), lambda: (align(2), align(3)), None, None, turn, logits,
                        None, None, None]

            def gates_T(c):
                pe.wait_ge(rt, 4 * c + 4)
                pe.sem_inc(passed, 1)
                for k in range(CH):
                    mm = nc.tensor.transpose(pC[:, S * k:S * k + S], cf[:, k, :], identb[:, :])
                mm.then_inc(cfT_ps, 1)

            def second(c, par, s):
                if s == 0:
                    pe.wait_ge(o_r, CH * c + CH)
                    for k in range(CH):
                        nc.tensor.matmul(pY[k], cfT[:, par, S * k:S * k + S], bias[:, :],
                                         start=(k % 2 == 0), stop=False, skip_group_check=True)
                pe.wait_ge(hl_r, NE * c + s + 1)
                for k in range(CH):
                    for a, b in ((0, 0), (0, 1), (1, 0)):
                        mm = nc.tensor.matmul(pY[k], halves[:, s % 3, a, S * k:S * k + S], w2[:, b, (s - 1) % NE, :],
                                              start=False, stop=(s == NE - 1 and a == 1), skip_group_check=True)
                    if s == NE - 1:
                        mm.then_inc(y_r, 1)
                if s < NE - 1:
                    mm.then_inc(y_e, 1)

            def ffn(c, par, parts):
                for s in range(NE):
                    pe.wait_ge(h_r, NE * c + s + 1)
                    if s == 0:
                        pe.wait_ge(x2_r, CH * c + CH + 2)
                    mm = products(pH[hbuf(par, s)], lambda half, i: w1[:, half, i, (s - 1) % NE, :],
                                  lambda half, i: x2T[:, par, KT * half + i, :])
                    mm.then_inc(h_ps, 1)
                    if s >= 1:
                        if s == 1:
                            pe.wait_ge(cfT_r, c + 2)
                        if s >= 2 or not first_chunk(c):
                            pe.wait_ge(hs_r, E * c + s - 1)
                        nc.tensor.matmul(pCb[(s - 1) % 2], sel3[:, s - 1, :], cfT[0:3 * E, par, :],
                                         start=True, stop=True).then_inc(cb_ps, 1)
                    if s >= 2:
                        second(c, par, s - 2)
                    elif not first_chunk(c):
                        second(c - 1, 1 - par, NE + s - 2)
                    if s == 0:
                        gates_T(c)
                    if parts:
                        parts[s]()

            pe.wait_ge(vTc, 2)
            pe.wait_ge(w_split, 9)
            pe.wait_ge(b_in, 16 * 9)
            schedule(pe, lambda c, par: [f or (lambda: None) for f in front(c, par)], ffn)
            second(NCH - 1, 1, NE - 2)
            second(NCH - 1, 1, NE - 1)

        @block.vector
        def _(dve):
            def hold():
                dve.sem_inc(passed, 1)

            for s_, n_ in ((xnT_r, 2), (cT_r, 2), (dst_r, CH), (d2_r, CH), (h_r, 2), (hs_r, 1),
                           (o_r, CH), (x2_r, 2), (cfT_r, 1), (mins, 1)):
                dve.sem_inc(s_, n_)
            dve.sem_inc(o_out, 16)
            nc.vector.memset(arenaD[:, :], BIG).then_inc(dall_init, 1)
            dve.wait_ge(consts, 4)
            nc.vector.tensor_scalar(qidx[:, :], pidx[:, :], 32 - LANES, None, ALU.bitwise_and).then_inc(dstep, 1)
            dve.wait_ge(dstep, 1)
            nc.vector.tensor_copy(qf[:, :], qidx[:, :]).then_inc(dstep, 1)
            dve.wait_ge(dstep, 2)
            nc.vector.tensor_scalar(edgeD[:, :], qf[:, :], 0.0, BIG, ALU.is_equal, ALU.mult).then_inc(dstep, 1)
            nc.vector.tensor_scalar(edgeR[:, :], qf[:, :], 0.0, BIG, ALU.not_equal, ALU.mult).then_inc(dstep, 1)
            nc.vector.tensor_scalar(base[:, :], qf[:, :], (W - 2.0 * S * LAG) / LANES, None, ALU.mult).then_inc(dstep, 1)
            nc.vector.memset(R[:, :, :], BIG).then_inc(dstep, 1)
            nc.vector.memset(M[:, :, :], BIG).then_inc(dstep, 1)
            nc.vector.memset(left[:, :, :], 0.0).then_inc(dstep, 1)
            nc.vector.tensor_copy(identb[:, :], ident[:, :]).then_inc(dstep, 1)
            nc.vector.tensor_copy(identh[:, :], ident[:, :]).then_inc(dstep, 1)
            nc.vector.memset(cf[:, :, :], 1.0).then_inc(dstep, 1)
            nc.vector.memset(VH[:, :], 0.0).then_inc(dstep, 1)
            nc.vector.tensor_copy(pf[:, :], pidx[:, :]).then_inc(dstep, 1)
            dve.wait_ge(dstep, 13)
            nc.vector.tensor_scalar(isE[:, :], pf[:, :], float(E), None, ALU.is_equal).then_inc(dstep, 1)
            nc.vector.tensor_scalar(notE[:, :], pf[:, :], float(E), None, ALU.not_equal).then_inc(dstep, 1)
            dve.wait_ge(dall_init, 1)
            nc.vector.tensor_scalar(Dall[:, 0, :], Dall[:, 0, :], 0.0, edgeD[:, 0:1], ALU.mult,
                                    ALU.add).then_inc(dall_init, 1)
            nc.vector.tensor_copy(R[:, RING - 1, 0:1], edgeR[:, :]).then_inc(dstep, 1)
            nc.vector.memset(VH[:, S:S + 1], S - 1.0).then_inc(dstep, 1)
            def measure(c, par):
                dve.wait_ge(x_in[par], 8 * (c - par) + 16)
                hold()
                for k in range(CH):
                    nc.vector.bn_stats(st[:, k, :], row(xt, c, k)).then_inc(stats, 1)
                dve.wait_ge(stats, 2 * CH * c + CH)
                hold()
                for k in range(CH):
                    nc.vector.bn_aggr(mv[:, par, k, :], st[:, k, :]).then_inc(stats, 1)

            def normalise(c, par):
                dve.wait_ge(rs2, c + 1)
                hold()
                for k in range(CH):
                    if not isinstance(c, int) or c >= 2:
                        dve.wait_ge(xnT_r, CH * c + k - 5)
                    nc.vector.tensor_scalar(xn[:, par, k, :], row(xt, c, k), mv[:, par, k, 0:1], rstd2[:, par, k:k + 1],
                                            ALU.subtract, ALU.mult).then_inc(xn_r, 1)
                bbc = bb[:, bass.ds(CH * c, CH)]
                nc.vector.scalar_tensor_tensor(out=bbc, in0=mv[:, par, :, 1], scalar=float(DM), in1=rstd2[:, par, :],
                                               op0=ALU.mult, op1=ALU.mult).then_inc(bbs, 1)
                dve.wait_ge(bbs, 2 * c + 1)
                nc.vector.tensor_tensor(bbc, bbc, rstd2[:, par, :], ALU.mult).then_inc(bbs, 1)

            def guard(c):
                dve.wait_ge(bbs, 2 * c + 2)
                for k in range(CH):
                    dve.wait_ge(ab_r, CH * c + k + 1)
                    dve.wait_ge(dst_r, CH * c + k + 1)
                    nc.vector.tensor_scalar(d2[:, k, :], pAB[k], col(bb, c, k), 0.0, ALU.add,
                                            ALU.max).then_inc(d2_r, 1)

            measure(0, 0)
            normalise(0, 0)
            measure(1, 1)
            normalise(1, 1)
            measure(2, 0)
            with dve.Fori(0, NCH // 2 - 2) as n:
                for r in range(2):
                    normalise(2 * n + r + 2, r)
                    measure(2 * n + r + 3, 1 - r)
                    guard(2 * n + r)
            normalise(NCH - 2, 0)
            measure(NCH - 1, 1)
            guard(NCH - 4)
            normalise(NCH - 1, 1)
            for c in range(NCH - 3, NCH):
                guard(c)
            dve.wait_ge(consts, 10)
            nc.vector.tensor_scalar(iotaJ, iotaJ, base[:, 0:1], None, ALU.add).then_inc(dstep, 1)
            dve.wait_ge(dall, 16 * QB * QB)
            dve.wait_ge(dstep, 18)
            dve.sem_inc(costs, 1)
            nc.vector.tensor_tensor(DL[:, 0:W], R[:, RING - 1, 0:W], R[:, RING - 1, 1:W + 1], ALU.is_le).then_inc(flag, 1)

            def diagonal_flags(m):
                two = slice(2 * (m % 2), 2 * (m % 2) + 2)
                nc.vector.tensor_tensor(DL[:, W * (2 * m + 1):W * (2 * m + 3)].rearrange("p (t w) -> p t w", w=W),
                                        R[:, two, 0:W], R[:, two, 1:W + 1], ALU.is_le).then_inc(flag, 1)

            def left_flags(m):
                two = slice(2 * (m % 2), 2 * (m % 2) + 2)
                nc.vector.tensor_tensor(LF[:, W * (2 * m + 1):W * (2 * m + 3)].rearrange("p (t w) -> p t w", w=W),
                                        R[:, two, 0:W], M[:, two, 1:W + 1], ALU.is_lt).then_inc(flag, 1)

            for t in range(T):
                cur, prev, last = t % RING, (t - 1) % RING, (t + 1) % RING
                dve.wait_ge(costs, t + 1)
                nc.vector.tensor_tensor(M[:, cur, 1:W + 1], R[:, prev, 1:W + 1], R[:, prev, 0:W],
                                        ALU.min).then_inc(mins, 1)
                if t >= 2:
                    (left_flags if t % 2 else diagonal_flags)((t - 2) // 2)
                dve.wait_ge(mins, 2 * t + 2)
                nc.vector.tensor_tensor_scan(R[:, cur, :], M[:, cur, :], Dall[:, :, t], BIG, ALU.min,
                                             ALU.add).then_inc(costs, 1)
                if t % 2 and t >= 3:
                    dve.wait_ge(flag, t)
                nc.vector.stream_shuffle(M[:, last, 0:1], R[:, prev, W:W + 1], shift[1]).then_inc(mins, 1)
            dve.wait_ge(costs, T + 1)
            diagonal_flags(T // 2 - 1)
            left_flags(T // 2 - 1)
            dve.wait_ge(w_split, 9)
            dve.wait_ge(flag, T + 1)
            nc.vector.scalar_tensor_tensor(out=cand[:, W * TAIL:], in0=DL[:, W * TAIL:W * T], scalar=-0.75,
                                           in1=iotaJ[:, W * TAIL:], op0=ALU.mult, op1=ALU.add).then_inc(bulk, 1)
            dve.wait_ge(bulk, 1)
            nc.vector.scalar_tensor_tensor(out=cand[:, W * TAIL:], in0=LF[:, W * (TAIL + 1):W * (T + 1)], scalar=-1000.0,
                                           in1=cand[:, W * TAIL:], op0=ALU.mult, op1=ALU.add).then_inc(bulk, 1)
            dve.wait_ge(cand_r, 2 * NSEG)
            dve.wait_ge(bulk, 2)
            nc.vector.tensor_tensor_scan(cand, cand, cand, 0.0, ALU.max, ALU.max).then_inc(bulk, 1)
            dve.wait_ge(bulk, 3)
            for k in range(1, QB):
                nc.vector.stream_shuffle(left[:, k - 1, LAG * k:T], candv[:, 0:T - LAG * k, W - 1],
                                         shift[k]).then_inc(bulk, 1)
            dve.wait_ge(bulk, 3 + QB - 1)
            nc.vector.tensor_tensor(left[:, 0, :], left[:, 0, :], left[:, 1, :], ALU.max).then_inc(bulk, 1)
            dve.wait_ge(bulk, 7)
            nc.vector.tensor_tensor(left[:, 0, 0:CUT], left[:, 0, 0:CUT], left[:, 2, 0:CUT], ALU.max).then_inc(bulk, 1)
            nc.vector.tensor_tensor(V2[:, CUT:T, 0], left[:, 0, CUT:T], left[:, 2, CUT:T], ALU.max).then_inc(bulk, 1)
            dve.wait_ge(bulk, BEFORE)
            nc.vector.tensor_tensor(V2[:, CUT:T, 1:W + 1], candv[:, CUT:T, :],
                                    V2[:, CUT:T, 0:1].to_broadcast([P, T - CUT, W]), ALU.max).then_inc(dV_r, 1)
            dve.wait_ge(dV_r, 1)
            nc.vector.tensor_tensor(dVv[:, CUT:T, :], V2[:, CUT:T, 1:W + 1], V2[:, CUT:T, 0:W],
                                    ALU.subtract).then_inc(dV_r, 1)
            dve.sem_inc(walk, 1)
            READY = {1: 1, ROWS + 1: 2, 2 * ROWS + 1: 4, 4 * ROWS + 1: 8, 8 * ROWS + 1: 16, 16 * ROWS + 1: 24,
                     24 * ROWS + 1: 32}
            for i in range(S - 1, 0, -1):
                if i == S // 2:
                    dve.wait_ge(wscale_r, 2)
                    nc.vector.reciprocal(wback[:, :], wscale[:, :]).then_inc(prep_c, 1)
                if S - i in READY:
                    dve.wait_ge(tab_r, READY[S - i])
                dve.wait_ge(walk, S - i)
                nc.vector.scalar_tensor_tensor(out=junk[:, :], in0=iotaL[:, :], scalar=VH[:, i + 1:i + 2], in1=table[:, i, :],
                                               op0=ALU.is_le, op1=ALU.mult, accum_out=VH[:, i:i + 1]).then_inc(walk, 1)
            dve.wait_ge(walk, S)
            dve.sem_inc(walk, 1)
            dve.wait_ge(vT, 1)
            for tile, o in ((hiC, 0), (loC, P)):
                nc.vector.tensor_copy(tile[:, :].rearrange("p (g u) -> p g u", g=QB),
                                      pPrep[:, o:o + P].rearrange("p (g u) -> p g u", g=QB)[:, :, 0:LANES]).then_inc(vTc, 1)

            LINKS = 18

            def masks(c):
                for k in range(CH):
                    dve.wait_ge(low_r, CH * c + k + 1)
                    nc.vector.scalar_tensor_tensor(out=mask[:, k, :], in0=iotaS[:, :], scalar=col(hiC, c, k),
                                                   in1=row(lowm, c, k), op0=ALU.is_le,
                                                   op1=ALU.subtract).then_inc(mask_r, 1)

            def front(c, par):
                done = [0]

                def link(ins):
                    ins.then_inc(chain, 1)
                    done[0] += 1
                    dve.wait_ge(chain, LINKS * c + done[0])

                def add(k0):
                    dve.wait_ge(al, CH * c + k0 + 2)
                    two = xt[:, bass.ds(CH * c + k0, 2), :]
                    nc.vector.scalar_tensor_tensor(out=two, in0=bank[k0 // 2][:, :].rearrange("p (k d) -> p k d", k=2),
                                                   scalar=gtanh[:, 0:1], in1=two, op0=ALU.mult,
                                                   op1=ALU.add).then_inc(x1_r, 1)
                    dve.wait_ge(x1_r, 2 * c + k0 // 2 + 1)
                    hold()
                    for k in (k0, k0 + 1):
                        nc.vector.bn_stats(st[:, k, :], row(xt, c, k)).then_inc(st2, 1)

                def moments():
                    dve.wait_ge(st2, CH * c + CH)
                    hold()
                    for k in range(CH):
                        nc.vector.bn_aggr(mv[:, 0, k, :], st[:, k, :]).then_inc(mv2, 1)

                def norm():
                    dve.wait_ge(mv2, CH * c + CH)
                    dve.wait_ge(rs2, NCH + c + 1)
                    for k in range(CH):
                        nc.vector.tensor_scalar(xn2[:, k, :], row(xt, c, k), mv[:, 0, k, 0:1], rstd2[:, 0, k:k + 1],
                                                ALU.subtract, ALU.mult).then_inc(xn2_r, 1)

                def logit():
                    dve.wait_ge(lg_ps, c + 1)
                    nc.vector.scalar_tensor_tensor(out=lg[:, :, :], in0=pLg, scalar=wback[:, 1:2],
                                                   in1=ebias[:, :].unsqueeze(1).to_broadcast([P, CH, E]),
                                                   op0=ALU.mult, op1=ALU.add).then_inc(lg_r, 1)
                    dve.wait_ge(lg_r, 2 * c + 1)
                    nc.vector.scalar_tensor_tensor(out=mag[:, :, :], in0=lg[:, :, :], scalar=-1.0, in1=lg[:, :, :],
                                                   op0=ALU.mult, op1=ALU.max).then_inc(lg_r, 1)

                def soft():
                    dve.wait_ge(spa, 2 * c + 1)
                    link(nc.vector.tensor_scalar(usum[:, :, :], ex[:, :, :], 1.0, None, ALU.add))
                    link(nc.vector.scalar_tensor_tensor(out=uerr[:, :, :], in0=usum[:, :, :], scalar=1.0,
                                                        in1=ex[:, :, :], op0=ALU.subtract, op1=ALU.subtract))
                    dve.wait_ge(spa, 2 * c + 2)
                    link(nc.vector.tensor_tensor(ln[:, :, :], ln[:, :, :], uerr[:, :, :], ALU.subtract))
                    nc.vector.scalar_tensor_tensor(out=sp[:, :, :], in0=lg[:, :, :], scalar=0.0, in1=ln[:, :, :],
                                                   op0=ALU.max, op1=ALU.add).then_inc(spb, 1)

                def top(v, hot, n):
                    link(nc.vector.tensor_reduce(m1[:, n, :], v[:, :, :], AX.X, ALU.max))
                    link(nc.vector.tensor_tensor(eq[:, :, :], v[:, :, :], m1[:, n, :].unsqueeze(2).to_broadcast([P, CH, E]),
                                                 ALU.is_equal))
                    link(nc.vector.tensor_tensor(eq[:, :, :], eq[:, :, :], rank[:, :, :], ALU.mult))
                    link(nc.vector.tensor_reduce(i1[:, :], eq[:, :, :], AX.X, ALU.max))
                    link(nc.vector.tensor_tensor(hot[:, :, :], rank[:, :, :],
                                                 i1[:, :].unsqueeze(2).to_broadcast([P, CH, E]), ALU.is_equal))

                def first_choice():
                    dve.wait_ge(spb, c + 1)
                    top(sp, oh, 0)
                    link(nc.vector.scalar_tensor_tensor(out=a2[:, :, :], in0=oh[:, :, :], scalar=-BIG,
                                                        in1=sp[:, :, :], op0=ALU.mult, op1=ALU.add))

                def second_choice():
                    top(a2, oh2, 1)
                    dve.sem_inc(chosen, 1)

                def gating():
                    dve.wait_ge(pw, c + 1)
                    for n, hot in enumerate((oh, oh2)):
                        link(nc.vector.scalar_tensor_tensor(out=hot[:, :, :], in0=hot[:, :, :], scalar=hscale[:, 0:1],
                                                            in1=root[:, n, :].unsqueeze(2).to_broadcast([P, CH, E]),
                                                            op0=ALU.mult, op1=ALU.mult))
                    nc.vector.tensor_tensor(gate[:, :, :], oh[:, :, :], oh2[:, :, :], ALU.add).then_inc(rt, 1)
                    dve.wait_ge(rt, 4 * c + 1)
                    nc.vector.tensor_copy(cfb[:, :, 2:5, :],
                                          gate[:, :, :].unsqueeze(2).to_broadcast([P, CH, 3, E])).then_inc(rt, 1)
                    dve.wait_ge(rt, 4 * c + 2)
                    link(nc.vector.tensor_tensor(res[:, :, :], gate[:, :, :], cfb[:, :, 2, :], ALU.subtract))
                    nc.vector.tensor_copy(cfb[:, :, 1:6:4, :],
                                          res[:, :, :].unsqueeze(2).to_broadcast([P, CH, 2, E])).then_inc(rt, 1)
                    dve.wait_ge(rt, 4 * c + 3)
                    link(nc.vector.tensor_tensor(res[:, :, :], res[:, :, :], cfb[:, :, 1, :], ALU.subtract))
                    nc.vector.tensor_copy(cfb[:, :, 0, :], res[:, :, :]).then_inc(rt, 1)
                    assert done[0] == LINKS

                def next_masks():
                    if not isinstance(c, int) or c + 1 < NCH:
                        masks(c + 1)
                return [lambda: add(0), lambda: (add(2), moments()), norm, None, None,
                        lambda: (logit(), soft(), first_choice()), second_choice, gating, next_masks]

            def low(c, par, s):
                dve.wait_ge(hi2_r, NE * c + s + 1)
                if s == 0:
                    nc.vector.scalar_tensor_tensor(out=halves[:, 0, 1, :], in0=hid[:, par, :], scalar=hscale[:, 0:1],
                                                   in1=halves[:, 0, 0, :], op0=ALU.mult,
                                                   op1=ALU.subtract).then_inc(hl_r, 1)
                else:
                    nc.vector.tensor_tensor(halves[:, s % 3, 1, :], hsc[:, (s - 1) % 2, :], halves[:, s % 3, 0, :],
                                            ALU.subtract).then_inc(hl_r, 1)

            def results(c):
                dve.wait_ge(o_out, 16 * c + 16)
                for k in range(0, CH, 2):
                    dve.wait_ge(y_r, CH * c + k + 2)
                    nc.vector.scalar_tensor_tensor(out=ot[:, k:k + 2, :],
                                                   in0=bank[5 + k // 2][:, :].rearrange("p (k d) -> p k d", k=2),
                                                   scalar=outg[:, 0:1], in1=xt[:, bass.ds(CH * c + k, 2), :],
                                                   op0=ALU.mult, op1=ALU.add).then_inc(o_r, 2)

            def ffn(c, par, parts):
                for s in range(NE):
                    if s >= 1:
                        low(c, par, s - 1)
                        dve.wait_ge(h_r, NE * c + s + 3)
                        dve.wait_ge(cb_ps, E * c + s)
                        if s >= 3:
                            dve.wait_ge(hl_r, NE * c + s - 1)
                        elif not first_chunk(c):
                            dve.wait_ge(hl_r, NE * c + s - 2)
                        nc.vector.tensor_tensor(hsc[:, (s - 1) % 2, :], hid[:, hbuf(par, s), :], pCb[(s - 1) % 2],
                                                ALU.mult).then_inc(hs_r, 1)
                        if s == 1 and not first_chunk(c):
                            results(c - 1)
                    elif not first_chunk(c):
                        low(c - 1, 1 - par, NE - 1)
                    if parts:
                        parts[s]()

            dve.wait_ge(prep_c, 2)
            nc.vector.tensor_tensor(outg[:, :], gtanh[:, 1:2], wback[:, 3:4], ALU.mult).then_inc(prep_c, 1)
            masks(0)
            schedule(dve, lambda c, par: [f or (lambda: None) for f in front(c, par)], ffn)
            low(NCH - 1, 1, NE - 1)
            dve.wait_ge(prep_c, 3)
            results(NCH - 1)


_INS = ['x', 'ctx_1024', 'g_xattn', 'g_ffn', 'L0_ffn_routing_W', 'L0_ffn_expert_bias', 'L0_ffn_sW1', 'L0_ffn_sb1',
        'L0_ffn_sW2', 'L0_ffn_sb2', 'L0_ffn_rW1', 'L0_ffn_rb1', 'L0_ffn_rW2', 'L0_ffn_rb2']


def kernel(**inputs):
    import numpy as _np
    import concourse.bacc as _bacc
    from concourse import mybir as _mybir
    from concourse.bass_utils import run_bass_kernel_spmd as _run

    nc = _bacc.Bacc("TRN2", target_bir_lowering=False, num_devices=1)
    arrays, args = {}, []
    for name in _INS:
        a = _np.ascontiguousarray(inputs[name])
        arrays[f"in_{name}"] = a
        args.append(nc.dram_tensor(f"in_{name}", a.shape, _mybir.dt.from_np(a.dtype), kind="ExternalInput").ap())
    o = nc.dram_tensor("out_0", inputs["x"].shape, _mybir.dt.float32, kind="ExternalOutput").ap()
    build_kernel(nc, *args, o)
    r = _run(nc, [arrays], core_ids=[0])
    return r.results[0]["out_0"]
```
